# Optimizing a Trainium2 kernel written in Bass

```python
import numpy as np
import jax
import jax.numpy as jnp

def _softmax(x, axis=-1):
    return jax.nn.softmax(x, axis=axis)

def _gelu(x):
    return jax.nn.gelu(x, approximate=True)

def _silu(x):
    return jax.nn.silu(x)

def _sigmoid(x):
    return jax.nn.sigmoid(x)

def _layernorm(x, axis=-1, eps=1e-05):
    m = jnp.mean(x, axis=axis, keepdims=True)
    v = jnp.var(x, axis=axis, keepdims=True)
    return (x - m) / jnp.sqrt(v + eps)

def _scatter_add(tgt, idx, src, axis=0):
    return tgt.at[idx].add(src)

def _segment_sum(src, seg, n):
    return jax.ops.segment_sum(src, seg, n)
kernel_name = 'mk_adj_seq_d1_adj_r2_4a3624'

def setup_inputs(seed: int=0):
    np.random.seed(seed)
    _w = jnp.asarray

    def _rec_inputs():
        import jax
        import jax.numpy as jnp
        _gk = jax.random.key(seed)
        x = -0.0005207 + 1.001 * jax.random.normal(jax.random.fold_in(_gk, 1), (4096, 256), jnp.float32)
        _a = jax.random.bernoulli(jax.random.fold_in(_gk, 2), 0.00195312, (4096, 4096))
        _a = jnp.logical_or(_a, jnp.swapaxes(_a, -1, -2))
        _a = jnp.logical_or(_a, jnp.eye(4096, dtype=bool))
        adj = _a.astype(jnp.int32)
        return (x, adj)
    x, adj = _rec_inputs()

    def _L0_gnn_setup():
        import jax, jax.numpy as jnp
        import numpy as np
        N, DIM = (2048, 256)
        F_OUT = DIM // 8
        HID = int(DIM * 2.0)
        ALPHA = 0.2
        MASK_VAL = -9000000000000000.0

        def _layernorm(x, g, b, eps=1e-05):
            mu = x.mean(-1, keepdims=True)
            var = ((x - mu) ** 2).mean(-1, keepdims=True)
            return (x - mu) * jax.lax.rsqrt(var + eps) * g + b
        key = jax.random.key(seed)
        ks = jax.random.split(key, 8)
        x = jax.random.normal(ks[0], (N, DIM), jnp.float32)
        adj = jax.random.randint(ks[1], (N, N), 0, 2, jnp.int32)
        W = jax.random.normal(ks[2], (DIM, F_OUT), jnp.float32) * 0.1
        a = jax.random.normal(ks[3], (2 * F_OUT, 1), jnp.float32) * 0.1
        fc_w = jax.random.normal(ks[4], (DIM, F_OUT), jnp.float32) * 0.1
        fc_b = jnp.zeros((DIM,), jnp.float32)
        ln1_g = jnp.ones((DIM,), jnp.float32)
        ln1_b = jnp.zeros((DIM,), jnp.float32)
        ln2_g = jnp.ones((DIM,), jnp.float32)
        ln2_b = jnp.zeros((DIM,), jnp.float32)
        fc1_w = jax.random.normal(ks[5], (HID, DIM), jnp.float32) * 0.05
        fc1_b = jnp.zeros((HID,), jnp.float32)
        fc2_w = jax.random.normal(ks[6], (DIM, HID), jnp.float32) * 0.05
        fc2_b = jnp.zeros((DIM,), jnp.float32)
        return dict(x=x, adj=adj, W=W, a=a, fc_w=fc_w, fc_b=fc_b, ln1_g=ln1_g, ln1_b=ln1_b, ln2_g=ln2_g, ln2_b=ln2_b, fc1_w=fc1_w, fc1_b=fc1_b, fc2_w=fc2_w, fc2_b=fc2_b)
    _L0_gnn_all = _L0_gnn_setup()
    _L0_gnn_in = {k: v for k, v in _L0_gnn_all.items() if k in ('W', 'a', 'fc_w', 'fc_b', 'ln1_g', 'ln1_b', 'ln2_g', 'ln2_b', 'fc1_w', 'fc1_b', 'fc2_w', 'fc2_b')}
    del _L0_gnn_all
    return {'x': x, 'adj': adj, 'L0_gnn_W': _L0_gnn_in['W'], 'L0_gnn_a': _L0_gnn_in['a'], 'L0_gnn_fc_w': _L0_gnn_in['fc_w'], 'L0_gnn_fc_b': _L0_gnn_in['fc_b'], 'L0_gnn_ln1_g': _L0_gnn_in['ln1_g'], 'L0_gnn_ln1_b': _L0_gnn_in['ln1_b'], 'L0_gnn_ln2_g': _L0_gnn_in['ln2_g'], 'L0_gnn_ln2_b': _L0_gnn_in['ln2_b'], 'L0_gnn_fc1_w': _L0_gnn_in['fc1_w'], 'L0_gnn_fc1_b': _L0_gnn_in['fc1_b'], 'L0_gnn_fc2_w': _L0_gnn_in['fc2_w'], 'L0_gnn_fc2_b': _L0_gnn_in['fc2_b']}

def reference(x, adj, L0_gnn_W, L0_gnn_a, L0_gnn_fc_w, L0_gnn_fc_b, L0_gnn_ln1_g, L0_gnn_ln1_b, L0_gnn_ln2_g, L0_gnn_ln2_b, L0_gnn_fc1_w, L0_gnn_fc1_b, L0_gnn_fc2_w, L0_gnn_fc2_b):
    import jax
    import jax.numpy as jnp

    def _L0_gnn_ref(x, adj, W, a, fc_w, fc_b, ln1_g, ln1_b, ln2_g, ln2_b, fc1_w, fc1_b, fc2_w, fc2_b):
        import jax, jax.numpy as jnp
        import numpy as np
        N, DIM = (2048, 256)
        F_OUT = DIM // 8
        HID = int(DIM * 2.0)
        ALPHA = 0.2
        MASK_VAL = -9000000000000000.0

        def _layernorm(x, g, b, eps=1e-05):
            mu = x.mean(-1, keepdims=True)
            var = ((x - mu) ** 2).mean(-1, keepdims=True)
            return (x - mu) * jax.lax.rsqrt(var + eps) * g + b
        h = _layernorm(x, ln1_g, ln1_b)
        Wh = h @ W
        f_src = Wh @ a[:F_OUT, 0]
        f_dst = Wh @ a[F_OUT:, 0]
        e = f_src[:, None] + f_dst[None, :]
        e = jnp.where(e >= 0, e, ALPHA * e)
        att = jax.nn.softmax(jnp.where(adj > 0, e, MASK_VAL), axis=1)
        h_prime = att @ Wh
        attn_out = h_prime @ fc_w.T + fc_b
        x = x + attn_out
        h2 = _layernorm(x, ln2_g, ln2_b)
        m = jax.nn.gelu(h2 @ fc1_w.T + fc1_b, approximate=False)
        m = m @ fc2_w.T + fc2_b
        return x + m
    x = _L0_gnn_ref(x, adj, L0_gnn_W, L0_gnn_a, L0_gnn_fc_w, L0_gnn_fc_b, L0_gnn_ln1_g, L0_gnn_ln1_b, L0_gnn_ln2_g, L0_gnn_ln2_b, L0_gnn_fc1_w, L0_gnn_fc1_b, L0_gnn_fc2_w, L0_gnn_fc2_b)
    return x

_drawn_inputs = setup_inputs


def setup_inputs(seed=0):
    import zlib

    import numpy as np

    out = dict(_drawn_inputs(seed))
    spreads = {'L0_gnn_fc_b': (0.0, 0.1),
     'L0_gnn_ln1_g': (1.0, 0.2),
     'L0_gnn_ln1_b': (0.0, 0.1),
     'L0_gnn_ln2_g': (1.0, 0.2),
     'L0_gnn_ln2_b': (0.0, 0.1),
     'L0_gnn_fc1_b': (0.0, 0.1),
     'L0_gnn_fc2_b': (0.0, 0.1)}
    factors = {}
    for name, (base, spread) in spreads.items():
        noise = np.random.default_rng([zlib.crc32(name.encode()), seed]).standard_normal(out[name].shape)
        drawn = base * np.exp(spread * noise) if base else spread * noise
        out[name] = jnp.asarray(drawn.astype(out[name].dtype))
    for name, factor in factors.items():
        out[name] = (out[name] * factor).astype(out[name].dtype)
    return out
```

```python
from contextlib import ExitStack

import concourse.bass as bass
from concourse import mybir

ALU = mybir.AluOpType
ACT = mybir.ActivationFunctionType
AX = mybir.AxisListType
BF16 = mybir.dt.bfloat16
F32 = mybir.dt.float32
I32 = mybir.dt.int32

P = 128
N = 4096
DIM = 256
KT = DIM // P
F = 32
FE = F + 1
HID = 512
HT = HID // P
T = N // P
GT = 4
GR = GT * P
G = T // GT
UB = 4
U = T // UB
RING = 4
PARTS = 3
VC = PARTS * FE
EPS = 1e-5
ALPHA = 0.2
RSQRT_MAGIC = 0x5F3759DF
NEWTON = 3

ALL_UNITS = (1, 2, 4, 5, 7)
LN1_G, LN1_B, LN2_G, LN2_B, FC1_B = 0, 2, 4, 6, 8
PARAMS = 12


def at_least(engine, semaphore, value):
    if not isinstance(value, int) or value > 0:
        engine.wait_ge(semaphore, value)


def build(nc, x, adj_t, w, w_t, a2, fc_wt, fc1_wt, fc2_wt, fc2_b, params, out):
    with ExitStack() as ctx:
        def sb(name, shape, dtype):
            return ctx.enter_context(nc.sbuf_tensor(name, shape, dtype))

        def sem(name):
            return ctx.enter_context(nc.semaphore(name))

        bank = [ctx.enter_context(nc.psum_tensor(f"bank{i}", [P, 512], F32)) for i in range(8)]
        acc = [bank[0:2], bank[2:4]]
        post = bank[4:8]

        ident = sb("ident", [P, P], F32)
        ones = sb("ones", [P, P], F32)
        par = sb("par", [P, PARAMS], F32)
        w_ext = sb("w_ext", [P, KT, F + 2], F32)
        wt_sb = sb("wt_sb", [F, DIM], F32)
        a2_sb = sb("a2_sb", [F, 2], F32)
        fc_sb = sb("fc_sb", [FE, DIM], F32)
        fc1_sb = sb("fc1_sb", [P, KT, HID], F32)
        fc2_sb = sb("fc2_sb", [P, HT, DIM], F32)
        fc2b_sb = sb("fc2b_sb", [P, DIM], F32)

        x_sb = sb("x_sb", [P, T, DIM], F32)
        srow = sb("srow", [P, N], F32)
        wh = sb("wh", [P, T, FE], F32)
        sd = sb("sd", [P, 2, T], F32)
        neg_d = sb("neg_d", [P, T], F32)
        bd = sb("bd", [P, 2, T], F32)
        ac = sb("ac", [P, T, 2], F32)
        val = sb("val", [P, T, 3 * VC], BF16)
        wh_sum = sb("wh_sum", [P, FE], F32)
        stats = sb("stats", [P, T, 6], F32)
        mv = sb("mv", [P, T, 2], F32)
        rstd = sb("rstd", [P, T], F32)
        mv2 = sb("mv2", [P, GT, 2], F32)
        rstd2 = sb("rstd2", [P, GT], F32)
        nt = sb("nt", [P, 2, T], F32)
        ti = sb("ti", [P, T], I32)

        adj = sb("adj", [P, RING, UB * GR], I32)
        non = sb("non", [P, RING, UB, GR], BF16)
        pos = sb("pos", [P, RING, UB, GR], BF16)
        rest = sb("rest", [P, RING, UB, GR], BF16)
        xn = sb("xn", [P, GT, DIM], F32)
        x_t = sb("x_t", [P, KT, GR], F32)
        hid = sb("hid", [P, HT, GR], F32)
        mlp = sb("mlp", [P, GT, DIM], F32)
        red = sb("red", [P, GT, 2, FE], F32)
        scl = sb("scl", [P, GT, 2, FE], F32)
        num = sb("num", [P, GT, FE], F32)
        hp = sb("hp", [P, GT, P], F32)
        x1 = sb("x1", [P, GT, DIM], F32)
        res = sb("res", [P, GT, DIM], F32)
        hp_t = sb("hp_t", [FE, GR], F32)
        empty = sb("empty", [P, GT], F32)
        rden = sb("rden", [P, GT], F32)
        dg = sb("dg", [P, GT, P], F32)
        sm = sb("sm", [P, 2], F32)
        gmx = sb("gmx", [P, 2], F32)
        nb = sb("nb", [P, 2], F32)
        uu = sb("uu", [P, 3, T], F32)
        wsum = sb("wsum", [P, FE], F32)
        prod = hid[:, 0:3, :].rearrange("p a b -> p (a b)")[:, 0:T * FE].rearrange("p (t c) -> p t c", c=FE)
        left = mlp[:, :, :].rearrange("p a b -> p (a b)")
        prod2 = sb("prod2", [P, T, FE], F32)

        s_x = [sem(f"x_landed{i}") for i in range(4)]
        s_w = sem("weights_landed")
        s_w2 = sem("mlp_weights_landed")
        s_const = sem("constants_ready")
        s_stats = sem("stats_ready")
        s_step = sem("vector_step")
        s_wa = sem("w_a_done")
        s_wext = sem("w_ext_ready")
        s_rstd = sem("rstd_ready")
        s_xn1 = sem("ln1_rows_ready")
        s_xt1 = sem("ln1_transposed")
        s_xt1c = sem("ln1_transposed_copied")
        s_wh = sem("wh_done")
        s_whc = sem("wh_copied")
        s_dg = sem("diagonals_ready")
        s_srow = sem("source_row_done")
        s_srowc = sem("source_row_copied")
        s_mx = sem("maxima_ready")
        s_mxb = sem("maxima_spread")
        s_nb = sem("guard_ready")
        s_arg = sem("row_arguments_ready")
        s_exp = sem("exponentials_ready")
        s_prod = sem("products_ready")
        s_part = sem("parts_ready")
        s_wsum = sem("tile_sum_ready")
        s_whsum = sem("node_sum_done")
        s_whsumc = sem("node_sum_copied")
        s_adj = [sem(f"adj_landed{i}") for i in range(RING)]
        s_non = sem("non_ready")
        s_pos = sem("pos_ready")
        s_rest_v = sem("rest_by_vector")
        s_rest_s = sem("rest_by_scalar")
        s_mm = sem("unit_summed")
        s_cstep = sem("combine_step")
        s_comb = sem("sums_read")
        s_hp = sem("attention_ready")
        s_hpt = sem("attention_transposed")
        s_hptc = sem("attention_transposed_copied")
        s_fc = sem("fc_done")
        s_x1 = sem("residual_added")
        s_lstep = sem("ln2_step")
        s_ln2 = sem("ln2_statistics_ready")
        s_cen = sem("ln2_rows_centred")
        s_xn = sem("ln2_rows_ready")
        s_xt = sem("ln2_transposed")
        s_xtc = sem("ln2_transposed_copied")
        s_fc1 = sem("fc1_done")
        s_gelu = sem("gelu_done")
        s_fc2 = sem("fc2_done")
        s_mlpc = sem("mlp_copied")
        s_bias = sem("fc2_bias_added")
        s_out = sem("rows_finished")
        s_wrote = sem("rows_written")

        out_v = out.rearrange("(t p) d -> p t d", p=P)
        x_v = x.rearrange("(t p) d -> p t d", p=P)

        n_all = len(ALL_UNITS)
        n_vec = U - n_all

        def rests(g, k):
            by_scalar = sum(u <= k for u in ALL_UNITS)
            return n_vec * g + (k + 1 - by_scalar), n_all * g + by_scalar

        block = ctx.enter_context(nc.Block())

        @block.sync
        def _(sp):
            for c in range(4):
                sp.dma_start(x_sb[:, 8 * c:8 * c + 8, :], x_v[:, 8 * c:8 * c + 8, :]).then_inc(s_x[c], 16)

            def load(g, k):
                at_least(sp, s_non, U * g + k + 1 - RING)
                sp.dma_start(adj[:, k % RING, :], adj_t[g, k]).then_inc(s_adj[k % RING], 16)

            def store(p):
                sp.wait_ge(s_out, 2 * p + 2)
                sp.dma_start(out_v[:, bass.ts(p, GT), :], res[:]).then_inc(s_wrote, 16)

            for g in range(2):
                for k in range(U):
                    load(g, k)
            with sp.Fori(2, G) as g:
                for k in range(U):
                    load(g, k)
                    if k == 3:
                        store(g - 2)
            store(G - 2)
            store(G - 1)
            sp.wait_ge(s_wrote, 16 * G)

        @block.gpsimd
        def _(pool):
            nc.gpsimd.memset(ident[:], 0.0).then_inc(s_const, 1)
            nc.gpsimd.memset(ones[:], 1.0).then_inc(s_const, 1)
            nc.gpsimd.memset(wh[:, :, F:FE], 1.0).then_inc(s_const, 1)
            nc.gpsimd.memset(hp[:], 0.0).then_inc(s_const, 1)
            pool.wait_ge(s_const, 4)
            nc.gpsimd.affine_select(out=ident[:], in_=ident[:], compare_op=ALU.not_equal, fill=1.0, base=0,
                                    pattern=[[-1, P]], channel_multiplier=1).then_inc(s_const, 1)
            pool.wait_ge(s_const, 5)

            def diagonals(c):
                pool.wait_ge(s_whc, 2 * c + 2)
                at_least(pool, s_srow, c)
                nc.gpsimd.tensor_tensor(
                    dg[:], ident[:].unsqueeze(1).to_broadcast([P, GT, P]),
                    sd[:, 0, bass.ts(c, GT)].unsqueeze(2).to_broadcast([P, GT, P]), ALU.mult).then_inc(s_dg, 1)

            for c in range(G):
                diagonals(c)

            def rows(p):
                pool.wait_ge(s_ln2, p + 1)
                at_least(pool, s_xt, 2 * p)
                nc.gpsimd.tensor_tensor(xn[:], x1[:], mv2[:, :, 0:1].to_broadcast([P, GT, DIM]),
                                        ALU.subtract).then_inc(s_cen, 1)
                pool.wait_ge(s_cen, p + 1)
                nc.gpsimd.tensor_tensor(xn[:], xn[:], rstd2[:].unsqueeze(2).to_broadcast([P, GT, DIM]),
                                        ALU.mult).then_inc(s_xn, 1)
                at_least(pool, s_wrote, 16 * p)
                nc.gpsimd.tensor_tensor(res[:], x1[:], fc2b_sb[:].unsqueeze(1).to_broadcast([P, GT, DIM]),
                                        ALU.add).then_inc(s_bias, 1)
                pool.wait_ge(s_bias, p + 1)
                for h in range(2):
                    pool.wait_ge(s_mlpc, 2 * p + h + 1)
                    half = res[:, 2 * h:2 * h + 2, :]
                    nc.gpsimd.tensor_tensor(half, half, mlp[:, 2 * h:2 * h + 2, :], ALU.add).then_inc(s_out, 1)

            pool.wait_ge(s_w2, 16 * 4)
            with pool.Fori(0, G) as p:
                rows(p)

        @block.scalar
        def _(act):
            act.dma_start(par[:], params).then_inc(s_w, 16)
            act.dma_start(wt_sb[:], w_t).then_inc(s_w, 16)
            act.dma_start(a2_sb[:], a2).then_inc(s_w, 16)
            act.dma_start(w_ext[:, :, 0:F], w.rearrange("(k p) f -> p k f", p=P)).then_inc(s_w, 16)
            act.dma_start(fc_sb[:], fc_wt).then_inc(s_w2, 16)
            act.dma_start(fc1_sb[:], fc1_wt.rearrange("(k p) m -> p k m", p=P)).then_inc(s_w2, 16)
            act.dma_start(fc2_sb[:], fc2_wt.rearrange("(k p) m -> p k m", p=P)).then_inc(s_w2, 16)
            act.dma_start(fc2b_sb[:], fc2_b).then_inc(s_w2, 16)
            act.wait_ge(s_wa, 1)
            act.wait_ge(s_w, 64)
            nc.scalar.activation(w_ext[:, :, F:F + 2], post[0][:, 0:2 * KT].rearrange("p (k c) -> p k c", k=KT),
                                 ACT.Copy).then_inc(s_wext, 1)

            def ln1_copy(c):
                for k in range(KT):
                    act.wait_ge(s_xt1, KT * c + k + 1)
                    at_least(act, s_wh, c)
                    nc.scalar.activation(x_t[:, k, :], post[k][:], ACT.Identity, bias=par[:, LN1_B + k:LN1_B + k + 1],
                                         scale=par[:, LN1_G + k:LN1_G + k + 1]).then_inc(s_xt1c, 1)

            def source_copy(c):
                act.wait_ge(s_srow, c + 1)
                nc.scalar.activation(srow[:, bass.ts(c, GR)], post[3][:], ACT.Copy).then_inc(s_srowc, 1)

            for c in range(G):
                ln1_copy(c)
                if c > 0:
                    source_copy(c - 1)
            source_copy(G - 1)

            act.wait_ge(s_nb, 1)
            nc.scalar.activation(bd[:, 0, :], sd[:, 1, :], ACT.Exp, bias=nb[:, 0:1]).then_inc(s_exp, 1)
            nc.scalar.activation(bd[:, 1, :], sd[:, 1, :], ACT.Exp, bias=nb[:, 1:2], scale=ALPHA).then_inc(s_exp, 1)
            act.wait_ge(s_arg, 1)
            nc.scalar.activation(ac[:, :, 0], uu[:, 0, :], ACT.Exp).then_inc(s_exp, 1)
            nc.scalar.activation(ac[:, :, 1], uu[:, 1, :], ACT.Exp).then_inc(s_exp, 1)

            def mask(g, k):
                n = U * g + k
                act.wait_ge(s_adj[k % RING], 16 * ((U // RING) * g + k // RING + 1))
                at_least(act, s_pos, n + 1 - RING)
                if k >= RING:
                    at_least(act, s_rest_v, rests(g, k - RING)[0])
                else:
                    at_least(act, s_rest_v, rests(g - 1, k - RING + U)[0])
                nc.scalar.activation(non[:, k % RING, :, :], adj[:, k % RING, :].rearrange("p (b i) -> p b i", b=UB),
                                     ACT.Relu, bias=1.0, scale=-1.0).then_inc(s_non, 1)
                if k in ALL_UNITS:
                    act.wait_ge(s_non, n + 1)
                    at_least(act, s_mm, n + 1 - RING)
                    nc.scalar.activation(rest[:, k % RING, :, :], non[:, k % RING, :, :], ACT.Relu,
                                         bias=1.0, scale=-1.0).then_inc(s_rest_s, 1)

            def hp_copy(p):
                act.wait_ge(s_hpt, p + 1)
                at_least(act, s_fc, 2 * p)
                nc.scalar.activation(hp_t[:], post[0][0:FE, :], ACT.Copy).then_inc(s_hptc, 1)

            def ln2_copy(p, k):
                act.wait_ge(s_xt, KT * p + k + 1)
                at_least(act, s_fc1, HT * p)
                nc.scalar.activation(x_t[:, k, :], post[3 if k == 0 else 0][:], ACT.Identity,
                                     bias=par[:, LN2_B + k:LN2_B + k + 1],
                                     scale=par[:, LN2_G + k:LN2_G + k + 1]).then_inc(s_xtc, 1)

            def gelu(p, m):
                act.wait_ge(s_fc1, HT * p + m + 1)
                at_least(act, s_fc2, 2 * p)
                nc.scalar.activation(hid[:, m, :], post[(1 + m) % 4][:], ACT.Gelu,
                                     bias=par[:, FC1_B + m:FC1_B + m + 1]).then_inc(s_gelu, 1)

            def mlp_copy(p, h):
                act.wait_ge(s_fc2, 2 * p + h + 1)
                at_least(act, s_out, 2 * p)
                nc.scalar.activation(mlp[:, 2 * h:2 * h + 2, :], post[1 + h][:].rearrange("p (t d) -> p t d", d=DIM),
                                     ACT.Copy).then_inc(s_mlpc, 1)

            POST = {1: [hp_copy], 4: [lambda p: ln2_copy(p, 0), lambda p: ln2_copy(p, 1)],
                    5: [lambda p: gelu(p, 0), lambda p: gelu(p, 1)], 6: [lambda p: gelu(p, 2), lambda p: gelu(p, 3)],
                    7: [lambda p: mlp_copy(p, 0), lambda p: mlp_copy(p, 1)]}
            act.wait_ge(s_part, 1)

            def group(g, first):
                for k in range(U):
                    mask(g, k)
                    if not first:
                        for step in POST.get(k, []):
                            step(g - 1)

            group(0, True)
            with act.Fori(1, G) as g:
                group(g, False)
            for k in range(U):
                for step in POST.get(k, []):
                    step(G - 1)

        @block.vector
        def _(dve):
            class_count = [0]

            def step(ins):
                class_count[0] += 1
                ins.then_inc(s_step, 1)
                dve.wait_ge(s_step, class_count[0])

            def rsqrt(link, var, y, a, i):
                v = nt_v = a[1]
                link(nc.vector.tensor_scalar(v, var, EPS, None, ALU.add))
                link(nc.vector.tensor_scalar(i, v.bitcast(I32), 1, None, ALU.logical_shift_right))
                link(nc.vector.tensor_scalar(y.bitcast(I32), i, -1.0, float(RSQRT_MAGIC), ALU.mult, ALU.add))
                for _ in range(NEWTON):
                    link(nc.vector.tensor_tensor(a[0], y, y, ALU.mult))
                    link(nc.vector.scalar_tensor_tensor(a[0], a[0], -0.5, v, ALU.mult, ALU.mult))
                    link(nc.vector.scalar_tensor_tensor(y, a[0], 1.5, y, ALU.add, ALU.mult))

            for c in range(4):
                dve.wait_ge(s_x[c], 16)
                for t in range(8 * c, 8 * c + 8):
                    ins = nc.vector.bn_stats(stats[:, t, :], x_sb[:, t, :])
                step(ins)
                for t in range(8 * c, 8 * c + 8):
                    ins = nc.vector.bn_aggr(mv[:, t, :], stats[:, t, :])
                step(ins)
            rsqrt(step, mv[:, :, 1], rstd[:], (nt[:, 0, :], nt[:, 1, :]), ti[:])

            def ln1_rows(c):
                at_least(dve, s_xt1, KT * c)
                for u in range(GT):
                    t = GT * c + u
                    ins = nc.vector.tensor_scalar(xn[:, u, :], x_sb[:, t, :], mv[:, t, 0:1], rstd[:, t:t + 1],
                                                  ALU.subtract, ALU.mult)
                ins.then_inc(s_xn1, 1)

            def wh_copy(c):
                dve.wait_ge(s_wh, c + 1)
                if c == 0:
                    dve.wait_ge(s_const, 5)
                got = post[2][:, 0:GT * (F + 2)].rearrange("p (t f) -> p t f", t=GT)
                nc.vector.tensor_copy(wh[:, GT * c:GT * c + GT, 0:F], got[:, :, 0:F]).then_inc(s_whc, 1)
                nc.vector.tensor_copy(sd[:, :, GT * c:GT * c + GT].rearrange("p s t -> p t s"),
                                      got[:, :, F:F + 2]).then_inc(s_whc, 1)

            for c in range(G):
                ln1_rows(c)
                if c > 0:
                    wh_copy(c - 1)
            wh_copy(G - 1)
            dve.wait_ge(s_whc, 2 * G)

            step(nc.vector.tensor_scalar(neg_d[:], sd[:, 1, :], -1.0, None, ALU.mult))
            nc.vector.tensor_reduce(sm[:, 0:1], sd[:, 1, :], AX.X, ALU.max)
            step(nc.vector.tensor_reduce(sm[:, 1:2], neg_d[:], AX.X, ALU.max))
            dve.wait_ge(s_srow, G)
            for i in range(2):
                ins = nc.vector.tensor_scalar(dg[:, i, :], ident[:], sm[:, i:i + 1], None, ALU.mult)
            ins.then_inc(s_mx, 1)
            step(nc.vector.tensor_reduce(wsum[:], wh[:].rearrange("p t c -> p c t"), AX.X, ALU.add))
            nc.vector.tensor_copy(wsum[:, 0:1], wsum[:, 0:1]).then_inc(s_wsum, 1)
            dve.wait_ge(s_mxb, 1)
            step(nc.vector.tensor_reduce(gmx[:], post[0][:, 0:2 * P].rearrange("p (a b) -> p a b", a=2), AX.X, ALU.max))
            nc.vector.tensor_scalar(nb[:, 0:1], gmx[:, 0:1], -1.0, None, ALU.mult)
            nc.vector.tensor_scalar(nb[:, 1:2], gmx[:, 0:1], -ALPHA, None, ALU.mult).then_inc(s_nb, 1)
            step(nc.vector.tensor_scalar(uu[:, 2, :], sd[:, 0, :], gmx[:, 0:1], None, ALU.add))
            step(nc.vector.scalar_tensor_tensor(nt[:, 0, :], uu[:, 2, :], ALPHA, uu[:, 2, :], ALU.mult, ALU.max))
            nc.vector.tensor_tensor(uu[:, 0, :], uu[:, 2, :], nt[:, 0, :], ALU.subtract)
            nc.vector.scalar_tensor_tensor(uu[:, 1, :], uu[:, 2, :], ALPHA, nt[:, 0, :], ALU.mult,
                                           ALU.subtract).then_inc(s_arg, 1)
            dve.wait_ge(s_exp, 2)
            pr = (prod, prod2[:])
            for i, base in enumerate((0, 2 * VC)):
                v = [val[:, :, base + FE * q:base + FE * (q + 1)] for q in range(PARTS)]
                step(nc.vector.tensor_tensor(pr[i], wh[:], bd[:, i, :].unsqueeze(2).to_broadcast([P, T, FE]), ALU.mult))
                for q in range(PARTS):
                    step(nc.vector.tensor_copy(v[q], pr[i]))
                    if q < PARTS - 1:
                        step(nc.vector.tensor_tensor(pr[i], pr[i], v[q], ALU.subtract))
            nc.vector.tensor_scalar(val[:, :, VC:2 * VC], val[:, :, 2 * VC:3 * VC], -1.0, None,
                                    ALU.mult).then_inc(s_part, 1)
            dve.wait_ge(s_whsum, 1)
            nc.vector.tensor_copy(wh_sum[:], post[1][:, 0:FE]).then_inc(s_whsumc, 1)
            dve.wait_ge(s_whsumc, 1)
            dve.wait_ge(s_exp, 4)
            dve.wait_ge(s_srowc, G)

            def masks(g, k):
                n = U * g + k
                dve.wait_ge(s_non, n + 1)
                at_least(dve, s_mm, n + 1 - RING)
                for b in range(UB):
                    j = UB * k + b
                    ins = nc.vector.scalar_tensor_tensor(pos[:, k % RING, b, :], srow[:, bass.ts(g, GR)],
                                                         neg_d[:, j:j + 1], non[:, k % RING, b, :],
                                                         ALU.is_ge, ALU.is_gt)
                ins.then_inc(s_pos, 1)
                if k not in ALL_UNITS:
                    dve.wait_ge(s_pos, n + 1)
                    nc.vector.tensor_tensor(rest[:, k % RING, :, :], pos[:, k % RING, :, :], non[:, k % RING, :, :],
                                            ALU.is_equal).then_inc(s_rest_v, 1)

            COMBINE = 7

            def combine(p, par_):
                count = [0]

                def link(ins):
                    count[0] += 1
                    ins.then_inc(s_cstep, 1)
                    dve.wait_ge(s_cstep, COMBINE * p + count[0])

                dve.wait_ge(s_mm, U * (p + 1))
                for h in range(2):
                    sums = acc[par_][h][:, 0:4 * VC].rearrange("p (s q c) -> p s c q", s=4, q=PARTS)
                    ins = nc.vector.tensor_reduce(
                        red[:, 2 * h:2 * h + 2, :, :].rearrange("p t s c -> p (t s) c"), sums, AX.X, ALU.add)
                    ins.then_inc(s_comb, 1)
                dve.wait_ge(s_comb, 2 * p + 2)
                link(nc.vector.tensor_tensor(
                    scl[:].rearrange("p t s c -> p (t s) c"), red[:].rearrange("p t s c -> p (t s) c"),
                    ac[:, bass.ts(p, GT), :].rearrange("p t s -> p (t s)").unsqueeze(2).to_broadcast([P, 2 * GT, FE]),
                    ALU.mult))
                link(nc.vector.tensor_tensor(num[:], scl[:, :, 0, :], scl[:, :, 1, :], ALU.add))
                link(nc.vector.tensor_scalar(empty[:], num[:, :, F], 0.0, None, ALU.is_equal))
                link(nc.vector.tensor_tensor(scl[:, :, 0, :], wh_sum[:].unsqueeze(1).to_broadcast([P, GT, FE]),
                                             empty[:].unsqueeze(2).to_broadcast([P, GT, FE]), ALU.mult))
                link(nc.vector.tensor_tensor(num[:], num[:], scl[:, :, 0, :], ALU.add))
                link(nc.vector.reciprocal(rden[:], num[:, :, F]))
                at_least(dve, s_hpt, p)
                nc.vector.tensor_tensor(hp[:, :, 0:FE], num[:], rden[:].unsqueeze(2).to_broadcast([P, GT, FE]),
                                        ALU.mult).then_inc(s_hp, 1)
                dve.wait_ge(s_hp, p + 1)
                link(nc.vector.tensor_copy(empty[:, 0:1], rden[:, 0:1]))
                assert count[0] == COMBINE

            LN2 = 2 + 3 + 3 * NEWTON

            def residual(p):
                count = [0]

                def link(ins):
                    count[0] += 1
                    ins.then_inc(s_lstep, 1)
                    dve.wait_ge(s_lstep, LN2 * p + count[0])

                for h in range(2):
                    dve.wait_ge(s_fc, 2 * p + h + 1)
                    at_least(dve, s_bias, p)
                    nc.vector.tensor_tensor(x1[:, 2 * h:2 * h + 2, :], x_sb[:, bass.ds(GT * p + 2 * h, 2), :],
                                            post[1 + h][:].rearrange("p (t d) -> p t d", d=DIM),
                                            ALU.add).then_inc(s_x1, 1)
                dve.wait_ge(s_x1, 2 * p + 2)
                for u in range(GT):
                    ins = nc.vector.bn_stats(stats[:, u, :], x1[:, u, :])
                link(ins)
                nc.vector.tensor_copy(sm[:, 0:1], sm[:, 1:2])
                for u in range(GT):
                    ins = nc.vector.bn_aggr(mv2[:, u, :], stats[:, u, :])
                link(ins)
                rsqrt(link, mv2[:, :, 1], rstd2[:], (nt[:, 0, 0:GT], nt[:, 1, 0:GT]),
                      ti[:, 0:GT])
                assert count[0] == LN2
                nc.vector.tensor_copy(empty[:, 0:1], rden[:, 0:1]).then_inc(s_ln2, 1)

            def group(g, parity, first):
                for k in range(U):
                    masks(g, k)
                    if not first:
                        if k == 0:
                            combine(g - 1, 1 - parity)
                        if k == 2:
                            residual(g - 1)

            group(0, 0, True)
            with dve.Fori(1, G - 1, 2) as g:
                group(g, 1, False)
                group(g + 1, 0, False)
            group(G - 1, 1, False)
            combine(G - 1, 1)
            residual(G - 1)

        @block.tensor
        def _(pe):
            pe.wait_ge(s_w, 64)
            for k in range(KT):
                ins = nc.tensor.matmul(post[0][:, 2 * k:2 * k + 2], wt_sb[:, P * k:P * k + P], a2_sb[:],
                                       start=True, stop=True)
            ins.then_inc(s_wa, 1)
            pe.wait_ge(s_const, 5)

            def ln1_transpose(c):
                pe.wait_ge(s_xn1, c + 1)
                if c == 0:
                    pe.wait_ge(s_wext, 1)
                at_least(pe, s_xt1c, KT * c)
                for k in range(KT):
                    for u in range(GT):
                        ins = nc.tensor.transpose(post[k][:, P * u:P * u + P], xn[:, u, P * k:P * k + P], ident[:])
                    ins.then_inc(s_xt1, 1)

            def project(c):
                pe.wait_ge(s_xt1c, KT * c + KT)
                at_least(pe, s_whc, 2 * c)
                for u in range(GT):
                    for k in range(KT):
                        ins = nc.tensor.matmul(post[2][:, (F + 2) * u:(F + 2) * (u + 1)], x_t[:, k, P * u:P * u + P],
                                               w_ext[:, k, :], start=(k == 0), stop=(k == KT - 1))
                ins.then_inc(s_wh, 1)

            def source_row(c):
                pe.wait_ge(s_dg, c + 1)
                at_least(pe, s_srowc, c)
                nc.tensor.matmul(post[3][:], ones[:], dg[:].rearrange("p u i -> p (u i)"), start=True,
                                 stop=True).then_inc(s_srow, 1)

            for c in range(G):
                ln1_transpose(c)
                project(c)
                if c > 0:
                    source_row(c - 1)
            source_row(G - 1)
            pe.wait_ge(s_mx, 1)
            nc.tensor.matmul(post[0][:, 0:2 * P], ones[:], dg[:, 0:2, :].rearrange("p u i -> p (u i)"), start=True,
                             stop=True).then_inc(s_mxb, 1)
            pe.wait_ge(s_wsum, 1)
            nc.tensor.matmul(post[1][:, 0:FE], ones[:], wsum[:], start=True, stop=True).then_inc(s_whsum, 1)
            pe.wait_ge(s_part, 1)
            pe.wait_ge(s_whsumc, 1)

            def unit(g, k, parity):
                by_vector, by_scalar = rests(g, k)
                pe.wait_ge(s_pos, U * g + k + 1)
                if k in ALL_UNITS:
                    pe.wait_ge(s_rest_s, by_scalar)
                else:
                    pe.wait_ge(s_rest_v, by_vector)
                if k == 0:
                    at_least(pe, s_comb, 2 * (g - 1))
                first_columns = 2 * VC if k in ALL_UNITS else VC
                for b in range(UB):
                    j = UB * k + b
                    for u in range(GT):
                        to, col = acc[parity][u // 2], 2 * VC * (u % 2)
                        nc.tensor.matmul(to[:, col:col + first_columns], pos[:, k % RING, b, P * u:P * u + P],
                                         val[:, j, 0:first_columns], start=(j == 0 and u % 2 == 0), stop=False,
                                         skip_group_check=True)
                        ins = nc.tensor.matmul(to[:, col + VC:col + 2 * VC], rest[:, k % RING, b, P * u:P * u + P],
                                               val[:, j, 2 * VC:3 * VC], start=False, stop=(j == T - 1),
                                               skip_group_check=True)
                ins.then_inc(s_mm, 1)

            def hp_transpose(p):
                pe.wait_ge(s_hp, p + 1)
                at_least(pe, s_gelu, HT * p)
                for u in range(GT):
                    ins = nc.tensor.transpose(post[0][:, P * u:P * u + P], hp[:, u, :], ident[:])
                ins.then_inc(s_hpt, 1)

            def fc(p):
                pe.wait_ge(s_hptc, p + 1)
                at_least(pe, s_mlpc, 2 * p)
                if isinstance(p, int) and p == 0:
                    pe.wait_ge(s_w2, 64)
                for u in range(GT):
                    ins = nc.tensor.matmul(post[1 + u // 2][:, DIM * (u % 2):DIM * (u % 2 + 1)],
                                           hp_t[:, P * u:P * u + P], fc_sb[:], start=True, stop=True)
                    if u % 2:
                        ins.then_inc(s_fc, 1)

            def ln2_transpose(p):
                pe.wait_ge(s_xn, p + 1)
                for k in range(KT):
                    for u in range(GT):
                        ins = nc.tensor.transpose(post[3 if k == 0 else 0][:, P * u:P * u + P],
                                                  xn[:, u, P * k:P * k + P], ident[:])
                    ins.then_inc(s_xt, 1)

            def fc1(p, m):
                pe.wait_ge(s_xtc, KT * p + KT)
                for k in range(KT):
                    ins = nc.tensor.matmul(post[(1 + m) % 4][:], fc1_sb[:, k, P * m:P * m + P], x_t[:, k, :],
                                           start=(k == 0), stop=(k == KT - 1))
                ins.then_inc(s_fc1, 1)

            def fc2(p, u):
                pe.wait_ge(s_gelu, HT * p + HT)
                for m in range(HT):
                    ins = nc.tensor.matmul(post[1 + u // 2][:, DIM * (u % 2):DIM * (u % 2 + 1)],
                                           hid[:, m, P * u:P * u + P], fc2_sb[:, m, :], start=(m == 0),
                                           stop=(m == HT - 1))
                if u % 2:
                    ins.then_inc(s_fc2, 1)

            POST = {1: [hp_transpose, fc], 4: [ln2_transpose], 5: [lambda p: fc1(p, 0), lambda p: fc1(p, 1)],
                    6: [lambda p: fc1(p, 2), lambda p: fc1(p, 3)],
                    7: [lambda p: fc2(p, 0), lambda p: fc2(p, 1), lambda p: fc2(p, 2), lambda p: fc2(p, 3)]}

            def group(g, parity, first):
                for k in range(U):
                    unit(g, k, parity)
                    if not first:
                        for step in POST.get(k, []):
                            step(g - 1)

            group(0, 0, True)
            pe.wait_ge(s_w2, 64)
            with pe.Fori(1, G - 1, 2) as g:
                group(g, 1, False)
                group(g + 1, 0, False)
            group(G - 1, 1, False)
            for k in range(U):
                for step in POST.get(k, []):
                    step(G - 1)


def kernel(x, adj, L0_gnn_W, L0_gnn_a, L0_gnn_fc_w, L0_gnn_fc_b, L0_gnn_ln1_g, L0_gnn_ln1_b, L0_gnn_ln2_g,
           L0_gnn_ln2_b, L0_gnn_fc1_w, L0_gnn_fc1_b, L0_gnn_fc2_w, L0_gnn_fc2_b):
    import numpy as np
    import concourse.bacc as bacc
    from concourse.bass_utils import run_bass_kernel_spmd as run

    nc = bacc.Bacc("TRN2", target_bir_lowering=False, num_devices=1)

    def columns(v):
        return np.asarray(v).reshape(-1, P).T

    adj_t = np.asarray(adj).reshape(G, GR, U, UB, P).transpose(0, 2, 4, 3, 1).reshape(G, U, P, UB * GR)
    arrays = {
        "x": x,
        "adj_t": adj_t,
        "w": L0_gnn_W,
        "w_t": np.asarray(L0_gnn_W).T,
        "a2": np.asarray(L0_gnn_a).reshape(2, F).T,
        "fc_wt": np.concatenate([np.asarray(L0_gnn_fc_w).T, np.asarray(L0_gnn_fc_b)[None, :]]),
        "fc1_wt": np.asarray(L0_gnn_fc1_w).T,
        "fc2_wt": np.asarray(L0_gnn_fc2_w).T,
        "fc2_b": np.broadcast_to(np.asarray(L0_gnn_fc2_b), (P, DIM)),
        "params": np.concatenate([columns(v) for v in (L0_gnn_ln1_g, L0_gnn_ln1_b, L0_gnn_ln2_g, L0_gnn_ln2_b,
                                                       L0_gnn_fc1_b)], axis=1),
    }
    arrays = {k: np.ascontiguousarray(v) for k, v in arrays.items()}
    dts = {"float32": F32, "int32": I32}
    aps = [nc.dram_tensor(k, v.shape, dts[v.dtype.name], kind="ExternalInput").ap() for k, v in arrays.items()]
    out = nc.dram_tensor("out", (N, DIM), F32, kind="ExternalOutput").ap()
    build(nc, *aps, out)
    r = run(nc, [arrays], core_ids=[0])
    return r.results[0]["out"]
```

```python
from contextlib import ExitStack

import concourse.bass as bass
from concourse import mybir

ALU = mybir.AluOpType
ACT = mybir.ActivationFunctionType
AX = mybir.AxisListType
BF16 = mybir.dt.bfloat16
F32 = mybir.dt.float32
I32 = mybir.dt.int32

P = 128
N = 4096
DIM = 256
KT = DIM // P
F = 32
FE = F + 1
HID = 512
HT = HID // P
T = N // P
GT = 4
GR = GT * P
G = T // GT
UB = 4
U = T // UB
RING = 4
PARTS = 3
VC = PARTS * FE
EPS = 1e-5
ALPHA = 0.2
RSQRT_MAGIC = 0x5F3759DF
NEWTON = 3

BY_SCALAR = (1, 2, 4, 5, 7)
LN1_G, LN1_B, LN2_G, LN2_B, FC1_B = 0, 2, 4, 6, 8
PARAMS = 12


def at_least(engine, semaphore, value):
    if not isinstance(value, int) or value > 0:
        engine.wait_ge(semaphore, value)


def build(nc, x, adj_t, w, w_t, a2, fc_wt, fc1_wt, fc2_wt, fc2_b, params, out):
    with ExitStack() as ctx:
        def sb(name, shape, dtype):
            return ctx.enter_context(nc.sbuf_tensor(name, shape, dtype))

        def sem(name):
            return ctx.enter_context(nc.semaphore(name))

        bank = [ctx.enter_context(nc.psum_tensor(f"bank{i}", [P, 512], F32)) for i in range(8)]
        acc = [bank[0:2], bank[2:4]]
        post = bank[4:8]

        ident = sb("ident", [P, P], F32)
        ones = sb("ones", [P, P], F32)
        par = sb("par", [P, PARAMS], F32)
        w_ext = sb("w_ext", [P, KT, F + 2], F32)
        wt_sb = sb("wt_sb", [F, DIM], F32)
        a2_sb = sb("a2_sb", [F, 2], F32)
        fc_sb = sb("fc_sb", [FE, DIM], F32)
        fc1_sb = sb("fc1_sb", [P, KT, HID], F32)
        fc2_sb = sb("fc2_sb", [P, HT, DIM], F32)
        fc2b_sb = sb("fc2b_sb", [P, DIM], F32)

        x_sb = sb("x_sb", [P, T, DIM], F32)
        srow = sb("srow", [P, N], F32)
        wh = sb("wh", [P, T, FE], F32)
        sd = sb("sd", [P, 2, T], F32)
        neg_d = sb("neg_d", [P, T], F32)
        bd = sb("bd", [P, 2, T], F32)
        ac = sb("ac", [P, T, 2], F32)
        val = sb("val", [P, T, 3 * VC], BF16)
        wh_sum = sb("wh_sum", [P, FE], F32)
        stats = sb("stats", [P, T, 6], F32)
        mv = sb("mv", [P, T, 2], F32)
        rstd = sb("rstd", [P, T], F32)
        mv2 = sb("mv2", [P, GT, 2], F32)
        rstd2 = sb("rstd2", [P, GT], F32)
        nt = sb("nt", [P, 2, T], F32)
        ti = sb("ti", [P, T], I32)

        adj = sb("adj", [P, RING, UB * GR], I32)
        non = sb("non", [P, RING, UB, GR], BF16)
        pos = sb("pos", [P, RING, UB, GR], BF16)
        every = sb("every", [P, RING, UB, GR], BF16)
        xn = sb("xn", [P, GT, DIM], F32)
        mlp = sb("mlp", [P, GT, DIM], F32)
        x_t = sb("x_t", [P, KT, GR], F32)
        hid = sb("hid", [P, HT, GR], F32)
        red = sb("red", [P, GT, 2, FE], F32)
        scl = sb("scl", [P, GT, 2, FE], F32)
        num = sb("num", [P, GT, FE], F32)
        hp = sb("hp", [P, GT, P], F32)
        x1 = sb("x1", [P, GT, DIM], F32)
        res = sb("res", [P, GT, DIM], F32)
        hp_t = sb("hp_t", [FE, GR], F32)
        empty = sb("empty", [P, GT], F32)
        rden = sb("rden", [P, GT], F32)
        dg = sb("dg", [P, GT, P], F32)
        sm = sb("sm", [P, 2], F32)
        gmx = sb("gmx", [P, 2], F32)
        nb = sb("nb", [P, 2], F32)
        uu = sb("uu", [P, 3, T], F32)
        wsum = sb("wsum", [P, FE], F32)
        prod = hid[:, 0:3, :].rearrange("p a b -> p (a b)")[:, 0:T * FE].rearrange("p (t c) -> p t c", c=FE)
        prod2 = sb("prod2", [P, T, FE], F32)

        s_x = [sem(f"x_landed{i}") for i in range(4)]
        s_w = sem("weights_landed")
        s_w2 = sem("mlp_weights_landed")
        s_const = sem("constants_ready")
        s_stats = sem("stats_ready")
        s_step = sem("vector_step")
        s_wa = sem("w_a_done")
        s_wext = sem("w_ext_ready")
        s_rstd = sem("rstd_ready")
        s_xn1 = sem("ln1_rows_ready")
        s_xt1 = sem("ln1_transposed")
        s_xt1c = sem("ln1_transposed_copied")
        s_wh = sem("wh_done")
        s_whc = sem("wh_copied")
        s_dg = sem("diagonals_ready")
        s_srow = sem("source_row_done")
        s_srowc = sem("source_row_copied")
        s_mx = sem("maxima_ready")
        s_mxb = sem("maxima_spread")
        s_nb = sem("guard_ready")
        s_arg = sem("row_arguments_ready")
        s_exp = sem("exponentials_ready")
        s_prod = sem("products_ready")
        s_part = sem("parts_ready")
        s_wsum = sem("tile_sum_ready")
        s_whsum = sem("node_sum_done")
        s_whsumc = sem("node_sum_copied")
        s_adj = [sem(f"adj_landed{i}") for i in range(RING)]
        s_non = sem("non_ready")
        s_pos = sem("pos_ready")
        s_every_v = sem("every_by_vector")
        s_every_s = sem("every_by_scalar")
        s_mm = sem("unit_summed")
        s_cstep = sem("combine_step")
        s_comb = sem("sums_read")
        s_hp = sem("attention_ready")
        s_hpt = sem("attention_transposed")
        s_hptc = sem("attention_transposed_copied")
        s_fc = sem("fc_done")
        s_x1 = sem("residual_added")
        s_lstep = sem("ln2_step")
        s_ln2 = sem("ln2_statistics_ready")
        s_cen = sem("ln2_rows_centred")
        s_xn = sem("ln2_rows_ready")
        s_xt = sem("ln2_transposed")
        s_xtc = sem("ln2_transposed_copied")
        s_fc1 = sem("fc1_done")
        s_gelu = sem("gelu_done")
        s_fc2 = sem("fc2_done")
        s_mlpc = sem("mlp_copied")
        s_bias = sem("fc2_bias_added")
        s_out = sem("rows_finished")
        s_wrote = sem("rows_written")

        out_v = out.rearrange("(t p) d -> p t d", p=P)
        x_v = x.rearrange("(t p) d -> p t d", p=P)

        n_scalar = len(BY_SCALAR)
        n_vector = U - n_scalar

        def everies(g, k):
            if k < 0:
                g, k = g - 1, k + U
            by_scalar = sum(u <= k for u in BY_SCALAR)
            return n_vector * g + (k + 1 - by_scalar), n_scalar * g + by_scalar

        block = ctx.enter_context(nc.Block())

        @block.sync
        def _(sp):
            for c in range(4):
                sp.dma_start(x_sb[:, 8 * c:8 * c + 8, :], x_v[:, 8 * c:8 * c + 8, :]).then_inc(s_x[c], 16)

            def load(g, k):
                at_least(sp, s_non, U * g + k + 1 - RING)
                sp.dma_start(adj[:, k % RING, :], adj_t[g, k]).then_inc(s_adj[k % RING], 16)

            def store(p):
                sp.wait_ge(s_out, 2 * p + 2)
                sp.dma_start(out_v[:, bass.ts(p, GT), :], res[:]).then_inc(s_wrote, 16)

            for g in range(3):
                for k in range(U):
                    load(g, k)
            with sp.Fori(3, G) as g:
                for k in range(U):
                    load(g, k)
                    if k == 3:
                        store(g - 3)
            store(G - 3)
            store(G - 2)
            store(G - 1)
            sp.wait_ge(s_wrote, 16 * G)

        @block.gpsimd
        def _(pool):
            nc.gpsimd.memset(ident[:], 0.0).then_inc(s_const, 1)
            nc.gpsimd.memset(ones[:], 1.0).then_inc(s_const, 1)
            nc.gpsimd.memset(wh[:, :, F:FE], 1.0).then_inc(s_const, 1)
            nc.gpsimd.memset(hp[:], 0.0).then_inc(s_const, 1)
            pool.wait_ge(s_const, 4)
            nc.gpsimd.affine_select(out=ident[:], in_=ident[:], compare_op=ALU.not_equal, fill=1.0, base=0,
                                    pattern=[[-1, P]], channel_multiplier=1).then_inc(s_const, 1)
            pool.wait_ge(s_const, 5)

            def diagonals(c):
                pool.wait_ge(s_whc, 2 * c + 2)
                at_least(pool, s_srow, c)
                nc.gpsimd.tensor_tensor(
                    dg[:], ident[:].unsqueeze(1).to_broadcast([P, GT, P]),
                    sd[:, 0, bass.ts(c, GT)].unsqueeze(2).to_broadcast([P, GT, P]), ALU.mult).then_inc(s_dg, 1)

            for c in range(G):
                diagonals(c)

            def normalise(p):
                pool.wait_ge(s_ln2, p + 1)
                at_least(pool, s_xt, KT * p)
                nc.gpsimd.tensor_tensor(xn[:], x1[:], mv2[:, :, 0:1].to_broadcast([P, GT, DIM]),
                                        ALU.subtract).then_inc(s_cen, 1)
                pool.wait_ge(s_cen, p + 1)
                nc.gpsimd.tensor_tensor(xn[:], xn[:], rstd2[:].unsqueeze(2).to_broadcast([P, GT, DIM]),
                                        ALU.mult).then_inc(s_xn, 1)

            def add_bias(p):
                at_least(pool, s_wrote, 16 * p)
                nc.gpsimd.tensor_tensor(res[:], x1[:], fc2b_sb[:].unsqueeze(1).to_broadcast([P, GT, DIM]),
                                        ALU.add).then_inc(s_bias, 1)

            def add_mlp(p):
                pool.wait_ge(s_bias, p + 1)
                for h in range(2):
                    pool.wait_ge(s_mlpc, 2 * p + h + 1)
                    half = res[:, 2 * h:2 * h + 2, :]
                    nc.gpsimd.tensor_tensor(half, half, mlp[:, 2 * h:2 * h + 2, :], ALU.add).then_inc(s_out, 1)

            pool.wait_ge(s_w2, 16 * 4)
            normalise(0)
            add_bias(0)
            with pool.Fori(1, G) as p:
                normalise(p)
                add_mlp(p - 1)
                add_bias(p)
            add_mlp(G - 1)

        @block.scalar
        def _(act):
            act.dma_start(par[:], params).then_inc(s_w, 16)
            act.dma_start(wt_sb[:], w_t).then_inc(s_w, 16)
            act.dma_start(a2_sb[:], a2).then_inc(s_w, 16)
            act.dma_start(w_ext[:, :, 0:F], w.rearrange("(k p) f -> p k f", p=P)).then_inc(s_w, 16)
            act.dma_start(fc_sb[:], fc_wt).then_inc(s_w2, 16)
            act.dma_start(fc1_sb[:], fc1_wt.rearrange("(k p) m -> p k m", p=P)).then_inc(s_w2, 16)
            act.dma_start(fc2_sb[:], fc2_wt.rearrange("(k p) m -> p k m", p=P)).then_inc(s_w2, 16)
            act.dma_start(fc2b_sb[:], fc2_b).then_inc(s_w2, 16)
            act.wait_ge(s_wa, 1)
            act.wait_ge(s_w, 64)
            nc.scalar.activation(w_ext[:, :, F:F + 2], post[0][:, 0:2 * KT].rearrange("p (k c) -> p k c", k=KT),
                                 ACT.Copy).then_inc(s_wext, 1)

            def ln1_copy(c):
                for k in range(KT):
                    act.wait_ge(s_xt1, KT * c + k + 1)
                    at_least(act, s_wh, c)
                    nc.scalar.activation(x_t[:, k, :], post[k][:], ACT.Identity, bias=par[:, LN1_B + k:LN1_B + k + 1],
                                         scale=par[:, LN1_G + k:LN1_G + k + 1]).then_inc(s_xt1c, 1)

            def source_copy(c):
                act.wait_ge(s_srow, c + 1)
                nc.scalar.activation(srow[:, bass.ts(c, GR)], post[3][:], ACT.Copy).then_inc(s_srowc, 1)

            for c in range(G):
                ln1_copy(c)
                if c > 0:
                    source_copy(c - 1)
            source_copy(G - 1)

            act.wait_ge(s_nb, 1)
            nc.scalar.activation(bd[:, 0, :], sd[:, 1, :], ACT.Exp, bias=nb[:, 0:1]).then_inc(s_exp, 1)
            nc.scalar.activation(bd[:, 1, :], sd[:, 1, :], ACT.Exp, bias=nb[:, 1:2], scale=ALPHA).then_inc(s_exp, 1)
            act.wait_ge(s_arg, 1)
            nc.scalar.activation(ac[:, :, 0], uu[:, 0, :], ACT.Exp).then_inc(s_exp, 1)
            nc.scalar.activation(ac[:, :, 1], uu[:, 1, :], ACT.Exp).then_inc(s_exp, 1)

            def mask(g, k):
                n = U * g + k
                act.wait_ge(s_adj[k % RING], 16 * ((U // RING) * g + k // RING + 1))
                at_least(act, s_pos, n + 1 - RING)
                at_least(act, s_every_v, everies(g, k - RING)[0])
                nc.scalar.activation(non[:, k % RING, :, :], adj[:, k % RING, :].rearrange("p (b i) -> p b i", b=UB),
                                     ACT.Relu, bias=1.0, scale=-1.0).then_inc(s_non, 1)
                if k in BY_SCALAR:
                    act.wait_ge(s_non, n + 1)
                    at_least(act, s_mm, n + 1 - RING)
                    nc.scalar.activation(every[:, k % RING, :, :], non[:, k % RING, :, :], ACT.Relu,
                                         bias=1.0, scale=-1.0).then_inc(s_every_s, 1)

            def hp_copy(p):
                act.wait_ge(s_hpt, p + 1)
                at_least(act, s_fc, 2 * p)
                nc.scalar.activation(hp_t[:], post[0][0:FE, :], ACT.Copy).then_inc(s_hptc, 1)

            def ln2_copy(p, k):
                act.wait_ge(s_xt, KT * p + k + 1)
                nc.scalar.activation(x_t[:, k, :], post[k][:], ACT.Identity,
                                     bias=par[:, LN2_B + k:LN2_B + k + 1],
                                     scale=par[:, LN2_G + k:LN2_G + k + 1]).then_inc(s_xtc, 1)

            def gelu(p, m):
                act.wait_ge(s_fc1, HT * p + m + 1)
                nc.scalar.activation(hid[:, m, :], post[2 + m % 2][:], ACT.Gelu,
                                     bias=par[:, FC1_B + m:FC1_B + m + 1]).then_inc(s_gelu, 1)

            def mlp_copy(p, h):
                act.wait_ge(s_fc2, 2 * p + h + 1)
                act.wait_ge(s_bias, p + 1)
                nc.scalar.activation(mlp[:, 2 * h:2 * h + 2, :], post[2 + h][:].rearrange("p (t d) -> p t d", d=DIM),
                                     ACT.Copy).then_inc(s_mlpc, 1)

            act.wait_ge(s_part, 1)

            def group(g, one, two):
                for k in range(U):
                    if g is not None:
                        mask(g, k)
                    if one is not None and k == 4:
                        hp_copy(one)
                    if two is not None:
                        if k == 0:
                            ln2_copy(two, 0)
                            ln2_copy(two, 1)
                        if 1 <= k <= HT:
                            gelu(two, k - 1)
                        if k == U - 1:
                            mlp_copy(two, 0)
                            mlp_copy(two, 1)

            group(0, None, None)
            group(1, 0, None)
            with act.Fori(2, G, 2) as g:
                group(g, g - 1, g - 2)
                group(g + 1, g, g - 1)
            group(None, G - 1, G - 2)
            group(None, None, G - 1)

        @block.vector
        def _(dve):
            class_count = [0]

            def step(ins):
                class_count[0] += 1
                ins.then_inc(s_step, 1)
                dve.wait_ge(s_step, class_count[0])

            def rsqrt(link, var, y, a, i):
                v = nt_v = a[1]
                link(nc.vector.tensor_scalar(v, var, EPS, None, ALU.add))
                link(nc.vector.tensor_scalar(i, v.bitcast(I32), 1, None, ALU.logical_shift_right))
                link(nc.vector.tensor_scalar(y.bitcast(I32), i, -1.0, float(RSQRT_MAGIC), ALU.mult, ALU.add))
                for _ in range(NEWTON):
                    link(nc.vector.tensor_tensor(a[0], y, y, ALU.mult))
                    link(nc.vector.scalar_tensor_tensor(a[0], a[0], -0.5, v, ALU.mult, ALU.mult))
                    link(nc.vector.scalar_tensor_tensor(y, a[0], 1.5, y, ALU.add, ALU.mult))

            for c in range(4):
                dve.wait_ge(s_x[c], 16)
                for t in range(8 * c, 8 * c + 8):
                    ins = nc.vector.bn_stats(stats[:, t, :], x_sb[:, t, :])
                step(ins)
                for t in range(8 * c, 8 * c + 8):
                    ins = nc.vector.bn_aggr(mv[:, t, :], stats[:, t, :])
                step(ins)
            rsqrt(step, mv[:, :, 1], rstd[:], (nt[:, 0, :], nt[:, 1, :]), ti[:])

            def ln1_rows(c):
                at_least(dve, s_xt1, KT * c)
                for u in range(GT):
                    t = GT * c + u
                    ins = nc.vector.tensor_scalar(xn[:, u, :], x_sb[:, t, :], mv[:, t, 0:1], rstd[:, t:t + 1],
                                                  ALU.subtract, ALU.mult)
                ins.then_inc(s_xn1, 1)

            def wh_copy(c):
                dve.wait_ge(s_wh, c + 1)
                if c == 0:
                    dve.wait_ge(s_const, 5)
                got = post[2][:, 0:GT * (F + 2)].rearrange("p (t f) -> p t f", t=GT)
                nc.vector.tensor_copy(wh[:, GT * c:GT * c + GT, 0:F], got[:, :, 0:F]).then_inc(s_whc, 1)
                nc.vector.tensor_copy(sd[:, :, GT * c:GT * c + GT].rearrange("p s t -> p t s"),
                                      got[:, :, F:F + 2]).then_inc(s_whc, 1)

            for c in range(G):
                ln1_rows(c)
                if c > 0:
                    wh_copy(c - 1)
            wh_copy(G - 1)
            dve.wait_ge(s_whc, 2 * G)

            step(nc.vector.tensor_scalar(neg_d[:], sd[:, 1, :], -1.0, None, ALU.mult))
            nc.vector.tensor_reduce(sm[:, 0:1], sd[:, 1, :], AX.X, ALU.max)
            step(nc.vector.tensor_reduce(sm[:, 1:2], neg_d[:], AX.X, ALU.max))
            dve.wait_ge(s_srow, G)
            for i in range(2):
                ins = nc.vector.tensor_scalar(dg[:, i, :], ident[:], sm[:, i:i + 1], None, ALU.mult)
            ins.then_inc(s_mx, 1)
            step(nc.vector.tensor_reduce(wsum[:], wh[:].rearrange("p t c -> p c t"), AX.X, ALU.add))
            nc.vector.tensor_copy(wsum[:, 0:1], wsum[:, 0:1]).then_inc(s_wsum, 1)
            dve.wait_ge(s_mxb, 1)
            step(nc.vector.tensor_reduce(gmx[:], post[0][:, 0:2 * P].rearrange("p (a b) -> p a b", a=2), AX.X, ALU.max))
            nc.vector.tensor_scalar(nb[:, 0:1], gmx[:, 0:1], -1.0, None, ALU.mult)
            nc.vector.tensor_scalar(nb[:, 1:2], gmx[:, 0:1], -ALPHA, None, ALU.mult).then_inc(s_nb, 1)
            step(nc.vector.tensor_scalar(uu[:, 2, :], sd[:, 0, :], gmx[:, 0:1], None, ALU.add))
            step(nc.vector.scalar_tensor_tensor(nt[:, 0, :], uu[:, 2, :], ALPHA, uu[:, 2, :], ALU.mult, ALU.max))
            nc.vector.tensor_tensor(uu[:, 0, :], uu[:, 2, :], nt[:, 0, :], ALU.subtract)
            nc.vector.scalar_tensor_tensor(uu[:, 1, :], uu[:, 2, :], ALPHA, nt[:, 0, :], ALU.mult,
                                           ALU.subtract).then_inc(s_arg, 1)
            dve.wait_ge(s_exp, 2)
            pr = (prod, prod2[:])
            for i, base in enumerate((0, 2 * VC)):
                v = [val[:, :, base + FE * q:base + FE * (q + 1)] for q in range(PARTS)]
                step(nc.vector.tensor_tensor(pr[i], wh[:], bd[:, i, :].unsqueeze(2).to_broadcast([P, T, FE]), ALU.mult))
                for q in range(PARTS):
                    step(nc.vector.tensor_copy(v[q], pr[i]))
                    if q < PARTS - 1:
                        step(nc.vector.tensor_tensor(pr[i], pr[i], v[q], ALU.subtract))
            nc.vector.tensor_scalar(val[:, :, VC:2 * VC], val[:, :, 2 * VC:3 * VC], -1.0, None,
                                    ALU.mult).then_inc(s_part, 1)
            dve.wait_ge(s_whsum, 1)
            nc.vector.tensor_copy(wh_sum[:], post[1][:, 0:FE]).then_inc(s_whsumc, 1)
            dve.wait_ge(s_whsumc, 1)
            dve.wait_ge(s_exp, 4)
            dve.wait_ge(s_srowc, G)

            def masks(g, k):
                n = U * g + k
                dve.wait_ge(s_non, n + 1)
                at_least(dve, s_mm, n + 1 - RING)
                for b in range(UB):
                    j = UB * k + b
                    ins = nc.vector.scalar_tensor_tensor(pos[:, k % RING, b, :], srow[:, bass.ts(g, GR)],
                                                         neg_d[:, j:j + 1], non[:, k % RING, b, :],
                                                         ALU.is_ge, ALU.is_gt)
                ins.then_inc(s_pos, 1)
                if k not in BY_SCALAR:
                    nc.vector.tensor_scalar(every[:, k % RING, :, :], non[:, k % RING, :, :], 0.0, None,
                                            ALU.is_equal).then_inc(s_every_v, 1)

            COMBINE = 7

            def combine(p, par_):
                count = [0]

                def link(ins):
                    count[0] += 1
                    ins.then_inc(s_cstep, 1)
                    dve.wait_ge(s_cstep, COMBINE * p + count[0])

                dve.wait_ge(s_mm, U * (p + 1))
                for h in range(2):
                    sums = acc[par_][h][:, 0:4 * VC].rearrange("p (s q c) -> p s c q", s=4, q=PARTS)
                    ins = nc.vector.tensor_reduce(
                        red[:, 2 * h:2 * h + 2, :, :].rearrange("p t s c -> p (t s) c"), sums, AX.X, ALU.add)
                    ins.then_inc(s_comb, 1)
                dve.wait_ge(s_comb, 2 * p + 2)
                link(nc.vector.tensor_tensor(
                    scl[:].rearrange("p t s c -> p (t s) c"), red[:].rearrange("p t s c -> p (t s) c"),
                    ac[:, bass.ts(p, GT), :].rearrange("p t s -> p (t s)").unsqueeze(2).to_broadcast([P, 2 * GT, FE]),
                    ALU.mult))
                link(nc.vector.tensor_tensor(num[:], scl[:, :, 0, :], scl[:, :, 1, :], ALU.add))
                link(nc.vector.tensor_scalar(empty[:], num[:, :, F], 0.0, None, ALU.is_equal))
                link(nc.vector.tensor_tensor(scl[:, :, 0, :], wh_sum[:].unsqueeze(1).to_broadcast([P, GT, FE]),
                                             empty[:].unsqueeze(2).to_broadcast([P, GT, FE]), ALU.mult))
                link(nc.vector.tensor_tensor(num[:], num[:], scl[:, :, 0, :], ALU.add))
                link(nc.vector.reciprocal(rden[:], num[:, :, F]))
                at_least(dve, s_hpt, p)
                nc.vector.tensor_tensor(hp[:, :, 0:FE], num[:], rden[:].unsqueeze(2).to_broadcast([P, GT, FE]),
                                        ALU.mult).then_inc(s_hp, 1)
                dve.wait_ge(s_hp, p + 1)
                link(nc.vector.tensor_copy(empty[:, 0:1], rden[:, 0:1]))
                assert count[0] == COMBINE

            LN2 = 2 + 3 + 3 * NEWTON

            def residual(p):
                count = [0]

                def link(ins):
                    count[0] += 1
                    ins.then_inc(s_lstep, 1)
                    dve.wait_ge(s_lstep, LN2 * p + count[0])

                for h in range(2):
                    dve.wait_ge(s_fc, 2 * p + h + 1)
                    at_least(dve, s_bias, p)
                    nc.vector.tensor_tensor(x1[:, 2 * h:2 * h + 2, :], x_sb[:, bass.ds(GT * p + 2 * h, 2), :],
                                            post[h][:].rearrange("p (t d) -> p t d", d=DIM),
                                            ALU.add).then_inc(s_x1, 1)
                dve.wait_ge(s_x1, 2 * p + 2)
                for u in range(GT):
                    ins = nc.vector.bn_stats(stats[:, u, :], x1[:, u, :])
                link(ins)
                nc.vector.tensor_copy(sm[:, 0:1], sm[:, 1:2])
                for u in range(GT):
                    ins = nc.vector.bn_aggr(mv2[:, u, :], stats[:, u, :])
                link(ins)
                rsqrt(link, mv2[:, :, 1], rstd2[:], (nt[:, 0, 0:GT], nt[:, 1, 0:GT]),
                      ti[:, 0:GT])
                assert count[0] == LN2
                nc.vector.tensor_copy(empty[:, 0:1], rden[:, 0:1]).then_inc(s_ln2, 1)

            def group(g, parity, first):
                for k in range(U):
                    masks(g, k)
                    if not first:
                        if k == 1:
                            combine(g - 1, 1 - parity)
                        if k == 4:
                            residual(g - 1)

            group(0, 0, True)
            group(1, 1, False)
            with dve.Fori(2, G - 1, 2) as g:
                group(g, 0, False)
                group(g + 1, 1, False)
            combine(G - 1, 1)
            residual(G - 1)

        @block.tensor
        def _(pe):
            pe.wait_ge(s_w, 64)
            for k in range(KT):
                ins = nc.tensor.matmul(post[0][:, 2 * k:2 * k + 2], wt_sb[:, P * k:P * k + P], a2_sb[:],
                                       start=True, stop=True)
            ins.then_inc(s_wa, 1)
            pe.wait_ge(s_const, 5)

            def ln1_transpose(c):
                pe.wait_ge(s_xn1, c + 1)
                if c == 0:
                    pe.wait_ge(s_wext, 1)
                at_least(pe, s_xt1c, KT * c)
                for k in range(KT):
                    for u in range(GT):
                        ins = nc.tensor.transpose(post[k][:, P * u:P * u + P], xn[:, u, P * k:P * k + P], ident[:])
                    ins.then_inc(s_xt1, 1)

            def project(c):
                pe.wait_ge(s_xt1c, KT * c + KT)
                at_least(pe, s_whc, 2 * c)
                for u in range(GT):
                    for k in range(KT):
                        ins = nc.tensor.matmul(post[2][:, (F + 2) * u:(F + 2) * (u + 1)], x_t[:, k, P * u:P * u + P],
                                               w_ext[:, k, :], start=(k == 0), stop=(k == KT - 1))
                ins.then_inc(s_wh, 1)

            def source_row(c):
                pe.wait_ge(s_dg, c + 1)
                at_least(pe, s_srowc, c)
                nc.tensor.matmul(post[3][:], ones[:], dg[:].rearrange("p u i -> p (u i)"), start=True,
                                 stop=True).then_inc(s_srow, 1)

            for c in range(G):
                ln1_transpose(c)
                project(c)
                if c > 0:
                    source_row(c - 1)
            source_row(G - 1)
            pe.wait_ge(s_mx, 1)
            nc.tensor.matmul(post[0][:, 0:2 * P], ones[:], dg[:, 0:2, :].rearrange("p u i -> p (u i)"), start=True,
                             stop=True).then_inc(s_mxb, 1)
            pe.wait_ge(s_wsum, 1)
            nc.tensor.matmul(post[1][:, 0:FE], ones[:], wsum[:], start=True, stop=True).then_inc(s_whsum, 1)
            pe.wait_ge(s_part, 1)
            pe.wait_ge(s_whsumc, 1)

            def unit(g, k, parity):
                by_vector, by_scalar = everies(g, k)
                pe.wait_ge(s_pos, U * g + k + 1)
                if k in BY_SCALAR:
                    pe.wait_ge(s_every_s, by_scalar)
                else:
                    pe.wait_ge(s_every_v, by_vector)
                if k == 0:
                    at_least(pe, s_comb, 2 * (g - 1))
                for b in range(UB):
                    j = UB * k + b
                    for u in range(GT):
                        to, col = acc[parity][u // 2], 2 * VC * (u % 2)
                        nc.tensor.matmul(to[:, col:col + 2 * VC], pos[:, k % RING, b, P * u:P * u + P],
                                         val[:, j, 0:2 * VC], start=(j == 0 and u % 2 == 0), stop=False,
                                         skip_group_check=True)
                        ins = nc.tensor.matmul(to[:, col + VC:col + 2 * VC], every[:, k % RING, b, P * u:P * u + P],
                                               val[:, j, 2 * VC:3 * VC], start=False, stop=(j == T - 1),
                                               skip_group_check=True)
                ins.then_inc(s_mm, 1)

            def hp_transpose(p):
                pe.wait_ge(s_hp, p + 1)
                at_least(pe, s_xtc, KT * p)
                for u in range(GT):
                    ins = nc.tensor.transpose(post[0][:, P * u:P * u + P], hp[:, u, :], ident[:])
                ins.then_inc(s_hpt, 1)

            def fc(p):
                pe.wait_ge(s_hptc, p + 1)
                for u in range(GT):
                    ins = nc.tensor.matmul(post[u // 2][:, DIM * (u % 2):DIM * (u % 2 + 1)],
                                           hp_t[:, P * u:P * u + P], fc_sb[:], start=True, stop=True)
                    if u % 2:
                        ins.then_inc(s_fc, 1)

            def ln2_transpose(p):
                pe.wait_ge(s_xn, p + 1)
                for k in range(KT):
                    for u in range(GT):
                        ins = nc.tensor.transpose(post[k][:, P * u:P * u + P], xn[:, u, P * k:P * k + P], ident[:])
                    ins.then_inc(s_xt, 1)

            def fc1(p, m):
                pe.wait_ge(s_xtc, KT * p + KT)
                if m < 2:
                    at_least(pe, s_mlpc, 2 * p - 1 + m)
                else:
                    pe.wait_ge(s_gelu, HT * p + m - 1)
                for k in range(KT):
                    ins = nc.tensor.matmul(post[2 + m % 2][:], fc1_sb[:, k, P * m:P * m + P], x_t[:, k, :],
                                           start=(k == 0), stop=(k == KT - 1))
                ins.then_inc(s_fc1, 1)

            def fc2(p, u):
                pe.wait_ge(s_gelu, HT * p + HT)
                for m in range(HT):
                    ins = nc.tensor.matmul(post[2 + u // 2][:, DIM * (u % 2):DIM * (u % 2 + 1)],
                                           hid[:, m, P * u:P * u + P], fc2_sb[:, m, :], start=(m == 0),
                                           stop=(m == HT - 1))
                if u % 2:
                    ins.then_inc(s_fc2, 1)

            FC2_AT = {3: (0,), 4: (1, 2), 5: (3,)}

            def group(g, parity, one, two):
                for k in range(U):
                    if g is not None:
                        unit(g, k, parity)
                    if one is not None:
                        if k == 1:
                            hp_transpose(one)
                        if k == 2:
                            fc(one)
                        if k == 5:
                            ln2_transpose(one)
                    if two is not None:
                        if k < 2:
                            fc1(two, 2 + k)
                        for u in FC2_AT.get(k, ()):
                            fc2(two, u)
                    if one is not None and k >= 6:
                        fc1(one, k - 6)

            group(0, 0, None, None)
            pe.wait_ge(s_w2, 64)
            group(1, 1, 0, None)
            with pe.Fori(2, G, 2) as g:
                group(g, 0, g - 1, g - 2)
                group(g + 1, 1, g, g - 1)
            group(None, 0, G - 1, G - 2)
            group(None, 1, None, G - 1)


def kernel(x, adj, L0_gnn_W, L0_gnn_a, L0_gnn_fc_w, L0_gnn_fc_b, L0_gnn_ln1_g, L0_gnn_ln1_b, L0_gnn_ln2_g,
           L0_gnn_ln2_b, L0_gnn_fc1_w, L0_gnn_fc1_b, L0_gnn_fc2_w, L0_gnn_fc2_b):
    import numpy as np
    import concourse.bacc as bacc
    from concourse.bass_utils import run_bass_kernel_spmd as run

    nc = bacc.Bacc("TRN2", target_bir_lowering=False, num_devices=1)

    def columns(v):
        return np.asarray(v).reshape(-1, P).T

    adj_t = np.asarray(adj).reshape(G, GR, U, UB, P).transpose(0, 2, 4, 3, 1).reshape(G, U, P, UB * GR)
    arrays = {
        "x": x,
        "adj_t": adj_t,
        "w": L0_gnn_W,
        "w_t": np.asarray(L0_gnn_W).T,
        "a2": np.asarray(L0_gnn_a).reshape(2, F).T,
        "fc_wt": np.concatenate([np.asarray(L0_gnn_fc_w).T, np.asarray(L0_gnn_fc_b)[None, :]]),
        "fc1_wt": np.asarray(L0_gnn_fc1_w).T,
        "fc2_wt": np.asarray(L0_gnn_fc2_w).T,
        "fc2_b": np.broadcast_to(np.asarray(L0_gnn_fc2_b), (P, DIM)),
        "params": np.concatenate([columns(v) for v in (L0_gnn_ln1_g, L0_gnn_ln1_b, L0_gnn_ln2_g, L0_gnn_ln2_b,
                                                       L0_gnn_fc1_b)], axis=1),
    }
    arrays = {k: np.ascontiguousarray(v) for k, v in arrays.items()}
    dts = {"float32": F32, "int32": I32}
    aps = [nc.dram_tensor(k, v.shape, dts[v.dtype.name], kind="ExternalInput").ap() for k, v in arrays.items()]
    out = nc.dram_tensor("out", (N, DIM), F32, kind="ExternalOutput").ap()
    build(nc, *aps, out)
    r = run(nc, [arrays], core_ids=[0])
    return r.results[0]["out"]
```

```python
from contextlib import ExitStack, contextmanager

import concourse.bass as bass
from concourse import mybir

ALU = mybir.AluOpType
ACT = mybir.ActivationFunctionType
AX = mybir.AxisListType
BF16 = mybir.dt.bfloat16
F32 = mybir.dt.float32
I32 = mybir.dt.int32

P = 128
N = 4096
DIM = 256
KT = DIM // P
F = 32
FE = F + 1
HID = 512
HT = HID // P
T = N // P
GT = 4
GR = GT * P
G = T // GT
UB = 4
U = T // UB
RING = 4
PARTS = 3
VC = PARTS * FE
EPS = 1e-5
ALPHA = 0.2
RSQRT_MAGIC = 0x5F3759DF
NEWTON = 3
RSQRT = 4 * NEWTON
MAX_SPREAD = 60.0
NO_WEIGHT = 1e-30
MASKED = -9e15
UNBOUND = 3e38
LAG = 4
EARLY_MASKS = (5, 6)
CONSTANTS = 8
TB = 4

BY_SCALAR = (0, 2, 3, 4, 6, 7)
LN1_G, LN1_B, LN2_G, LN2_B, FC1_B = 0, 2, 4, 6, 8
PARAMS = 12


def at_least(engine, semaphore, value):
    if not isinstance(value, int) or value > 0:
        engine.wait_ge(semaphore, value)


def build(nc, x, adj_t, adj_rows, w, w_t, a2, fc_wt, fc1_wt, fc2_wt, fc2_b, params, out):
    with ExitStack() as ctx:
        def sb(name, shape, dtype):
            return ctx.enter_context(nc.sbuf_tensor(name, shape, dtype))

        def sem(name):
            return ctx.enter_context(nc.semaphore(name))

        bank = [ctx.enter_context(nc.psum_tensor(f"bank{i}", [P, 512], F32)) for i in range(8)]
        acc = [bank[0:2], bank[2:4]]
        post = bank[4:8]

        ident = sb("ident", [P, P], F32)
        ones = sb("ones", [P, P], F32)
        par = sb("par", [P, PARAMS], F32)
        w_ext = sb("w_ext", [P, KT, F + 2], F32)
        pick = sb("pick", [F + 2, P], F32)
        wt_sb = sb("wt_sb", [F, DIM], F32)
        a2_sb = sb("a2_sb", [F, 2], F32)
        fc_sb = sb("fc_sb", [FE, DIM], F32)
        fc1_sb = sb("fc1_sb", [P, KT, HID], F32)
        fc2_sb = sb("fc2_sb", [P, HT, DIM], F32)
        fc2b_sb = sb("fc2b_sb", [P, DIM], F32)

        x_sb = sb("x_sb", [P, T, DIM], F32)
        srow = sb("srow", [P, N], F32)
        wh = sb("wh", [P, T, FE], F32)
        sd = sb("sd", [P, 2, T], F32)
        neg_d = sb("neg_d", [P, T], F32)
        bd = sb("bd", [P, 2, T], F32)
        ac = sb("ac", [P, T, 2], F32)
        val = sb("val", [P, T, 3 * VC], BF16)
        wh_sum = sb("wh_sum", [P, FE], F32)
        stats = sb("stats", [P, T, 6], F32)
        mv = sb("mv", [P, T, 2], F32)
        rstd = sb("rstd", [P, T], F32)
        mv2 = sb("mv2", [P, GT, 2], F32)
        rstd2 = sb("rstd2", [P, GT], F32)
        nt = sb("nt", [P, 2, T], F32)

        adj = sb("adj", [P, RING, UB * GR], I32)
        non = sb("non", [P, RING, UB, GR], BF16)
        pos = sb("pos", [P, RING, UB, GR], BF16)
        rest = sb("rest", [P, RING, UB, GR], BF16)
        xn = sb("xn", [P, GT, DIM], F32)
        x_t = sb("x_t", [P, KT, GR], F32)
        hid = sb("hid", [P, HT, GR], F32)
        red = sb("red", [P, GT, 2, FE], F32)
        scl = sb("scl", [P, GT, 2, FE], F32)
        num = sb("num", [P, GT, FE], F32)
        hp = sb("hp", [P, GT, P], F32)
        x1 = sb("x1", [P, GT, DIM], F32)
        res = sb("res", [P, GT, DIM], F32)
        hp_t = sb("hp_t", [FE, GR], F32)
        empty = sb("empty", [P, GT], F32)
        rden = sb("rden", [P, GT], F32)
        dg = sb("dg", [P, GT, P], F32)
        sm = sb("sm", [P, 2], F32)
        gmx = sb("gmx", [P, 2], F32)
        nb = sb("nb", [P, 2], F32)
        uu = sb("uu", [P, 3, T], F32)
        wide = sb("wide", [P, 1], I32)
        row_adj = adj[:].rearrange("p (s a) n -> p s (a n)", s=2)
        score = pos[:].rearrange("p r b i -> p (r b i)").bitcast(F32)
        limit = non[:].rearrange("p r b i -> p (r b i)").bitcast(F32)
        score_t = rest[:].rearrange("p r b i -> p (r b i)").bitcast(F32)
        three_halves = sb("three_halves", [P, GT], F32)
        variance = sb("variance", [P, GT], F32)
        minus_half_v = sb("minus_half_v", [P, GT], F32)
        square = sb("square", [P, GT], F32)
        neg_max = sb("neg_max", [P, 2], F32)
        ln_rows = (xn, x1)
        ln_t = (x_t[:], res[:].rearrange("p a b -> p (a b)").rearrange("p (k i) -> p k i", k=KT))
        wh_t = pos[:].rearrange("p r b i -> p (r b i)").bitcast(F32)[0:F + 2, :].rearrange("p (c i) -> p c i", c=G)
        prod = hid[:, 0:3, :].rearrange("p a b -> p (a b)")[:, 0:T * FE].rearrange("p (t c) -> p t c", c=FE)
        prod2 = sb("prod2", [P, T, FE], F32)

        s_x = [sem(f"x_landed{i}") for i in range(G)]
        s_w = sem("weights_landed")
        s_w2 = sem("mlp_weights_landed")
        s_const = sem("constants_ready")
        s_stats = sem("stats_ready")
        s_step = sem("vector_step")
        s_wa = sem("w_a_done")
        s_wext = sem("w_ext_ready")
        s_xn1 = sem("ln1_rows_ready")
        s_xt1 = sem("ln1_transposed")
        s_xt1c = sem("ln1_transposed_copied")
        s_wh = sem("wh_done")
        s_whtc = sem("wh_transposed_copied")
        s_whp = sem("wh_projected")
        s_whc = sem("wh_copied")
        s_negd = sem("minus_f_dst_ready")
        s_srow = sem("source_row_done")
        s_srowc = sem("source_row_copied")
        s_mx = sem("maxima_ready")
        s_mxb = sem("maxima_spread")
        s_nb = sem("guard_ready")
        s_arg = sem("row_arguments_ready")
        s_exp = sem("exponentials_ready")
        s_left_b = sem("b_wh_left_ready")
        s_left_d = sem("d_wh_left_ready")
        s_part = sem("parts_ready")
        s_minus = sem("minus_parts_ready")
        s_whsum = sem("node_sum_done")
        s_whsumc = sem("node_sum_copied")
        s_wide = sem("spread_known")
        s_ediag = sem("exact_diagonals_ready")
        s_edst = sem("exact_f_dst_spread")
        s_edstc = sem("exact_f_dst_copied")
        s_erow = [sem(f"exact_adj_landed{i}") for i in range(2)]
        s_eread = sem("exact_adj_read")
        s_estep = sem("exact_step")
        s_emax = sem("exact_maximum_ready")
        s_eexp = sem("exact_exponentials_ready")
        s_etr = sem("exact_bank_transposed")
        s_etrc = sem("exact_bank_copied")
        s_efree = sem("exact_scores_used")
        s_esum = sem("exact_sums_done")
        s_adj = [sem(f"adj_landed{i}") for i in range(RING)]
        s_non = sem("non_ready")
        s_pos = sem("pos_ready")
        s_rest_v = sem("rest_by_vector")
        s_rest_s = sem("rest_by_scalar")
        s_mm = sem("unit_summed")
        s_cstep = sem("combine_step")
        s_comb = sem("sums_read")
        s_hp = sem("attention_ready")
        s_hpt = sem("attention_transposed")
        s_hptc = sem("attention_transposed_copied")
        s_fc = sem("fc_done")
        s_x1 = sem("residual_added")
        s_lstep = sem("ln2_step")
        s_ln2 = sem("ln2_statistics_ready")
        s_pstep = sem("rsqrt_step")
        s_cen = sem("ln2_rows_centred")
        s_xn = sem("ln2_rows_ready")
        s_xt = sem("ln2_transposed")
        s_xtc = sem("ln2_transposed_copied")
        s_fc1 = sem("fc1_done")
        s_gelu = sem("gelu_done")
        s_fc2 = sem("fc2_done")
        s_bias = sem("fc2_bias_added")
        s_out = sem("rows_finished")
        s_wrote = sem("rows_written")
        s_wrote_half = sem("half_of_last_rows_written")

        out_v = out.rearrange("(t p) d -> p t d", p=P)
        x_v = x.rearrange("(t p) d -> p t d", p=P)

        def turn_banks(c):
            return bank[0:2] if c > G - LAG and c % 2 else post[2:4]

        def turn_before(c):
            return c if c <= G - LAG else c - 1

        def part(i, q):
            base = 2 * VC * i + FE * q
            return val[:, :, base:base + FE]

        n_scalar = len(BY_SCALAR)
        n_vector = U - n_scalar

        def rests(g, k):
            if k < 0:
                g, k = g - 1, k + U
            by_scalar = sum(u <= k for u in BY_SCALAR)
            return n_vector * g + (k + 1 - by_scalar), n_scalar * g + by_scalar

        def read_wide(engine):
            engine.wait_ge(s_wide, 1)
            return engine.value_load(wide[0:1, 0:1], min_val=0, max_val=1)

        @contextmanager
        def exact_pass(engine, is_wide=None):
            if is_wide is None:
                is_wide = read_wide(engine)
            with engine.If(is_wide == 1):
                engine.wait_ge(s_wrote_half, 16)
                engine.wait_ge(s_wrote, 16 * G)
                yield
            with engine.Else():
                engine.wait_ge(s_wide, 1)

        block = ctx.enter_context(nc.Block())

        @block.sync
        def _(sp):
            for c in range(G):
                sp.dma_start(x_sb[:, GT * c:GT * c + GT, :], x_v[:, GT * c:GT * c + GT, :]).then_inc(s_x[c], 16)

            def load(g, k):
                at_least(sp, s_non, U * g + k + 1 - RING)
                sp.dma_start(adj[:, k % RING, :], adj_t[g, k]).then_inc(s_adj[k % RING], 16)

            def store(p):
                sp.wait_ge(s_out, 2 * p + 2)
                sp.dma_start(out_v[:, bass.ts(p, GT), :], res[:]).then_inc(s_wrote, 16)

            for g in range(3):
                for k in range(U):
                    load(g, k)
            with sp.Fori(3, G) as g:
                for k in range(U):
                    load(g, k)
                    if k == 3:
                        store(g - 3)
            store(G - 3)
            store(G - 2)
            is_wide = read_wide(sp)
            for h in range(2):
                half = slice(GT * (G - 1) + 2 * h, GT * (G - 1) + 2 * h + 2)
                sp.wait_ge(s_out, 2 * (G - 1) + h + 1)
                sp.dma_start(out_v[:, half, :], res[:, 2 * h:2 * h + 2, :]).then_inc(s_wrote if h else s_wrote_half, 16)
            sp.wait_ge(s_wrote_half, 16)
            sp.wait_ge(s_wrote, 16 * G)

            with exact_pass(sp, is_wide):
                with sp.Fori(0, G) as q:
                    p = q + G
                    for u in range(GT):
                        sp.wait_ge(s_eread, GT * q + u + 1)
                        sp.dma_start(row_adj[:, u % 2, :], adj_rows[q, u]).then_inc(s_erow[u % 2], 16)
                    sp.wait_ge(s_out, 2 * p + 2)
                    sp.dma_start(out_v[:, bass.ts(q, GT), :], res[:]).then_inc(s_wrote, 16)
                sp.wait_ge(s_wrote, 16 * 2 * G)

        @block.gpsimd
        def _(pool):
            nc.gpsimd.memset(ident[:], 0.0).then_inc(s_const, 1)
            nc.gpsimd.memset(ones[:], 1.0).then_inc(s_const, 1)
            nc.gpsimd.memset(wh[:, :, F:FE], 1.0).then_inc(s_const, 1)
            nc.gpsimd.memset(hp[:], 0.0).then_inc(s_const, 1)
            nc.gpsimd.memset(pick[:], 0.0).then_inc(s_const, 1)
            pool.wait_ge(s_const, 5)
            nc.gpsimd.memset(three_halves[:], 1.5).then_inc(s_const, 1)
            pool.wait_ge(s_const, 6)
            nc.gpsimd.memset(pick[F:F + 1, :], 1.0).then_inc(s_const, 1)
            pool.wait_ge(s_const, 7)
            nc.gpsimd.affine_select(out=ident[:], in_=ident[:], compare_op=ALU.not_equal, fill=1.0, base=0,
                                    pattern=[[-1, P]], channel_multiplier=1).then_inc(s_const, 1)

            pool.wait_ge(s_exp, 2)
            pool.wait_ge(s_whc, 2 * G)
            nc.gpsimd.tensor_tensor(prod2[:], wh[:], bd[:, 1, :].unsqueeze(2).to_broadcast([P, T, FE]),
                                    ALU.mult).then_inc(s_left_d, 1)
            for q in range(PARTS - 1):
                pool.wait_ge(s_part, 2 * q + 2)
                pool.wait_ge(s_left_d, q + 1)
                nc.gpsimd.tensor_tensor(prod2[:], prod2[:], part(1, q), ALU.subtract).then_inc(s_left_d, 1)

            def normalise(p, before):
                count = [0]

                def link(ins):
                    count[0] += 1
                    ins.then_inc(s_pstep, 1)
                    pool.wait_ge(s_pstep, RSQRT * before + count[0])

                pool.wait_ge(s_ln2, p + 1)
                y, a, v = rstd2[:], square[:], minus_half_v[:]
                for _ in range(NEWTON):
                    link(nc.gpsimd.tensor_tensor(a, y, y, ALU.mult))
                    link(nc.gpsimd.tensor_tensor(a, a, v, ALU.mult))
                    link(nc.gpsimd.tensor_tensor(a, a, three_halves[:], ALU.add))
                    link(nc.gpsimd.tensor_tensor(y, a, y, ALU.mult))
                at_least(pool, s_xt, KT * p)
                nc.gpsimd.tensor_tensor(xn[:], x1[:], mv2[:, :, 0:1].to_broadcast([P, GT, DIM]),
                                        ALU.subtract).then_inc(s_cen, 1)
                pool.wait_ge(s_cen, before + 1)
                nc.gpsimd.tensor_tensor(xn[:], xn[:], rstd2[:].unsqueeze(2).to_broadcast([P, GT, DIM]),
                                        ALU.mult).then_inc(s_xn, 1)

            def add_bias(p):
                pool.wait_ge(s_x1, 2 * p + 2)
                at_least(pool, s_wrote, 16 * p)
                nc.gpsimd.tensor_tensor(res[:], x1[:], fc2b_sb[:].unsqueeze(1).to_broadcast([P, GT, DIM]),
                                        ALU.add).then_inc(s_bias, 1)

            pool.wait_ge(s_w2, 16 * 4)
            normalise(0, 0)
            add_bias(0)
            with pool.Fori(1, G - 1) as p:
                normalise(p, p)
                add_bias(p)
            add_bias(G - 1)

            with exact_pass(pool):
                with pool.Fori(G, 2 * G) as p:
                    normalise(p, p - 1)
                    add_bias(p)

        @block.scalar
        def _(act):
            act.dma_start(par[:], params).then_inc(s_w, 16)
            act.dma_start(wt_sb[:], w_t).then_inc(s_w, 16)
            act.dma_start(a2_sb[:], a2).then_inc(s_w, 16)
            act.dma_start(w_ext[:, :, 0:F], w.rearrange("(k p) f -> p k f", p=P)).then_inc(s_w, 16)
            act.dma_start(fc_sb[:], fc_wt).then_inc(s_w2, 16)
            act.dma_start(fc1_sb[:], fc1_wt.rearrange("(k p) m -> p k m", p=P)).then_inc(s_w2, 16)
            act.dma_start(fc2_sb[:], fc2_wt.rearrange("(k p) m -> p k m", p=P)).then_inc(s_w2, 16)
            act.dma_start(fc2b_sb[:], fc2_b).then_inc(s_w2, 16)
            act.wait_ge(s_wa, 1)
            act.wait_ge(s_w, 64)
            nc.scalar.activation(w_ext[:, :, F:F + 2], post[0][:, 0:2 * KT].rearrange("p (k c) -> p k c", k=KT),
                                 ACT.Copy).then_inc(s_wext, 1)

            def neighbours(g, k):
                n = U * g + k
                if k in BY_SCALAR:
                    act.wait_ge(s_non, n + 1)
                    at_least(act, s_mm, n + 1 - RING)
                    nc.scalar.activation(rest[:, k % RING, :, :], non[:, k % RING, :, :], ACT.Relu,
                                         bias=1.0, scale=-1.0).then_inc(s_rest_s, 1)

            def mask(g, k):
                n = U * g + k
                act.wait_ge(s_adj[k % RING], 16 * ((U // RING) * g + k // RING + 1))
                at_least(act, s_pos, n + 1 - RING)
                by_vector, by_scalar = rests(g, k - RING)
                at_least(act, s_rest_v, by_vector)
                at_least(act, s_rest_s, by_scalar)
                nc.scalar.activation(non[:, k % RING, :, :], adj[:, k % RING, :].rearrange("p (b i) -> p b i", b=UB),
                                     ACT.Relu, bias=1.0, scale=-1.0).then_inc(s_non, 1)
                if k > 0:
                    neighbours(g, k - 1)
                elif not (isinstance(g, int) and g == 0):
                    neighbours(g - 1, U - 1)

            def ln1_copy(c):
                at_least(act, s_whp, c - 1)
                for k in range(KT):
                    act.wait_ge(s_xt1, KT * c + k + 1)
                    nc.scalar.activation(ln_t[c % 2][:, k, :], bank[2 * (c % 2) + k][:], ACT.Identity,
                                         bias=par[:, LN1_B + k:LN1_B + k + 1],
                                         scale=par[:, LN1_G + k:LN1_G + k + 1]).then_inc(s_xt1c, 1)

            def projection_copy(c):
                act.wait_ge(s_whp, c + 1)
                nc.scalar.activation(wh_t[:, c, :], post[c % 2][0:F + 2, :], ACT.Copy).then_inc(s_whtc, 1)

            def source_copy(c):
                act.wait_ge(s_srow, c + 1)
                nc.scalar.activation(srow[:, bass.ts(c, GR)], turn_banks(c)[1][:], ACT.Copy).then_inc(s_srowc, 1)

            for c in range(G):
                ln1_copy(c)
                if c > 0:
                    projection_copy(c - 1)
                if c >= LAG:
                    source_copy(c - LAG)
                if 3 <= c < 5:
                    mask(0, c - 3)
            projection_copy(G - 1)
            for c in range(G - LAG, G):
                source_copy(c)
            mask(0, 2)
            mask(0, 3)

            act.wait_ge(s_nb, 1)
            nc.scalar.activation(bd[:, 0, :], sd[:, 1, :], ACT.Exp, bias=nb[:, 0:1]).then_inc(s_exp, 1)
            nc.scalar.activation(bd[:, 1, :], sd[:, 1, :], ACT.Exp, bias=nb[:, 1:2], scale=ALPHA).then_inc(s_exp, 1)
            act.wait_ge(s_arg, 1)
            nc.scalar.activation(ac[:, :, 0], uu[:, 0, :], ACT.Exp).then_inc(s_exp, 1)
            nc.scalar.activation(ac[:, :, 1], uu[:, 1, :], ACT.Exp).then_inc(s_exp, 1)
            for q in range(PARTS):
                for i in range(2):
                    act.wait_ge((s_left_b, s_left_d)[i], q + 1)
                    nc.scalar.activation(part(i, q), (prod, prod2[:])[i], ACT.Copy).then_inc(s_part, 1)

            def hp_copy(p):
                act.wait_ge(s_hpt, p + 1)
                at_least(act, s_fc, 2 * p)
                nc.scalar.activation(hp_t[:], post[0][0:FE, :], ACT.Copy).then_inc(s_hptc, 1)

            def ln2_copy(p, k):
                act.wait_ge(s_xt, KT * p + k + 1)
                nc.scalar.activation(x_t[:, k, :], post[k][:], ACT.Identity,
                                     bias=par[:, LN2_B + k:LN2_B + k + 1],
                                     scale=par[:, LN2_G + k:LN2_G + k + 1]).then_inc(s_xtc, 1)

            def gelu(p, m):
                act.wait_ge(s_fc1, HT * p + m + 1)
                nc.scalar.activation(hid[:, m, :], post[2 + m % 2][:], ACT.Gelu,
                                     bias=par[:, FC1_B + m:FC1_B + m + 1]).then_inc(s_gelu, 1)

            act.wait_ge(s_part, 2 * PARTS)

            def group(g, one, two):
                for k in range(U):
                    if g is not None and not (isinstance(g, int) and g == 0 and k < RING):
                        mask(g, k)
                    if one is not None and k == 4:
                        hp_copy(one)
                    if two is not None:
                        if k == 0:
                            ln2_copy(two, 0)
                            ln2_copy(two, 1)
                        if 1 <= k <= HT:
                            gelu(two, k - 1)

            group(0, None, None)
            group(1, 0, None)
            with act.Fori(2, G, 2) as g:
                group(g, g - 1, g - 2)
                group(g + 1, g, g - 1)
            neighbours(G - 1, U - 1)
            group(None, G - 1, G - 2)
            group(None, None, G - 1)

            with exact_pass(act):
                with act.Fori(0, G) as q:
                    for u in range(GT):
                        n = GT * q + u
                        act.wait_ge(s_emax, n + 1)
                        nc.scalar.activation(score, score, ACT.Exp, bias=neg_max[:, 1:2]).then_inc(s_eexp, 1)
                        for b in range(T // TB):
                            act.wait_ge(s_etr, T // TB * n + b + 1)
                            nc.scalar.activation(score_t[:, TB * P * b:TB * P * (b + 1)], acc[1][b % 2][:],
                                                 ACT.Copy).then_inc(s_etrc, 1)
                    p = q + G
                    hp_copy(p)
                    for k in range(KT):
                        ln2_copy(p, k)
                    for m in range(HT):
                        gelu(p, m)

        @block.vector
        def _(dve):
            steps = [0]

            def step(ins):
                steps[0] += 1
                ins.then_inc(s_step, 1)
                dve.wait_ge(s_step, steps[0])

            def rsqrt(var, y, a, v):
                step(nc.vector.tensor_scalar(v, var, EPS, None, ALU.add))
                step(nc.vector.tensor_scalar(y.bitcast(I32), v.bitcast(I32), -0.5, float(RSQRT_MAGIC), ALU.mult,
                                             ALU.add))
                newton(y, a, v)

            def newton(y, a, v):
                for _ in range(NEWTON):
                    step(nc.vector.tensor_tensor(a, y, y, ALU.mult))
                    step(nc.vector.scalar_tensor_tensor(a, a, -0.5, v, ALU.mult, ALU.mult))
                    step(nc.vector.scalar_tensor_tensor(y, a, 1.5, y, ALU.add, ALU.mult))

            def ln1_sums(c):
                dve.wait_ge(s_x[c], 16)
                for t in range(GT * c, GT * c + GT):
                    ins = nc.vector.bn_stats(stats[:, t, :], x_sb[:, t, :])
                ins.then_inc(s_stats, 1)

            def ln1_statistics(h):
                dve.wait_ge(s_stats, G // 2 * (h + 1))
                half = slice(T // 2 * h, T // 2 * (h + 1))
                for t in range(T // 2 * h, T // 2 * (h + 1)):
                    ins = nc.vector.bn_aggr(mv[:, t, :], stats[:, t, :])
                step(ins)
                rsqrt(mv[:, half, 1], rstd[:, half], nt[:, 0, half], nt[:, 1, half])

            def ln1_rows(c):
                at_least(dve, s_xt1, KT * (c - 1))
                for u in range(GT):
                    t = GT * c + u
                    ins = nc.vector.tensor_scalar(ln_rows[c % 2][:, u, :], x_sb[:, t, :], mv[:, t, 0:1], rstd[:, t:t + 1],
                                                  ALU.subtract, ALU.mult)
                ins.then_inc(s_xn1, 1)

            def wh_copy(c):
                dve.wait_ge(s_wh, c + 1)
                if c == 0:
                    dve.wait_ge(s_const, CONSTANTS)
                got = turn_banks(c)[0][:, 0:GT * (F + 2)].rearrange("p (t f) -> p t f", t=GT)
                nc.vector.tensor_copy(wh[:, GT * c:GT * c + GT, 0:F], got[:, :, 0:F]).then_inc(s_whc, 1)
                nc.vector.tensor_copy(sd[:, :, GT * c:GT * c + GT].rearrange("p s t -> p t s"),
                                      got[:, :, F:F + 2]).then_inc(s_whc, 1)
                dve.wait_ge(s_whc, 2 * c + 2)
                nc.vector.tensor_scalar(neg_d[:, GT * c:GT * c + GT], sd[:, 1, GT * c:GT * c + GT], -1.0, None,
                                        ALU.mult).then_inc(s_negd, 1)

            def masks(g, k):
                n = U * g + k
                dve.wait_ge(s_non, n + 1)
                at_least(dve, s_mm, n + 1 - RING)
                for b in range(UB):
                    j = UB * k + b
                    ins = nc.vector.scalar_tensor_tensor(pos[:, k % RING, b, :], srow[:, bass.ts(g, GR)],
                                                         neg_d[:, j:j + 1], non[:, k % RING, b, :],
                                                         ALU.is_ge, ALU.is_gt)
                ins.then_inc(s_pos, 1)
                if k not in BY_SCALAR:
                    dve.wait_ge(s_pos, n + 1)
                    nc.vector.tensor_tensor(rest[:, k % RING, :, :], pos[:, k % RING, :, :], non[:, k % RING, :, :],
                                            ALU.is_equal).then_inc(s_rest_v, 1)

            for c in range(G // 2):
                ln1_sums(c)
            ln1_statistics(0)
            for c in range(G // 2):
                ln1_rows(c)
                ln1_sums(G // 2 + c)
            ln1_statistics(1)
            for c in range(G // 2, G):
                ln1_rows(c)
                if c > LAG:
                    wh_copy(c - LAG - 1)
            for c in range(G - LAG - 1, G):
                wh_copy(c)
                for k in range(2):
                    if c == EARLY_MASKS[k]:
                        dve.wait_ge(s_srow, 2 * k + 2)
                        dve.wait_ge(s_srowc, 1)
                        dve.wait_ge(s_negd, k + 1)
                        masks(0, k)
            dve.wait_ge(s_whc, 2 * G)

            dve.wait_ge(s_negd, G)
            nc.vector.tensor_reduce(sm[:, 0:1], sd[:, 1, :], AX.X, ALU.max)
            step(nc.vector.tensor_reduce(sm[:, 1:2], neg_d[:], AX.X, ALU.max))
            for i in range(2):
                ins = nc.vector.tensor_scalar(dg[:, i, :], ident[:], sm[:, i:i + 1], None, ALU.mult)
            ins.then_inc(s_mx, 1)
            dve.wait_ge(s_mxb, 1)
            step(nc.vector.tensor_reduce(gmx[:], post[0][:, 0:2 * P].rearrange("p (a b) -> p a b", a=2), AX.X, ALU.max))
            nc.vector.tensor_scalar(nb[:, 0:1], gmx[:, 0:1], -1.0, None, ALU.mult)
            nc.vector.tensor_scalar(nb[:, 1:2], gmx[:, 0:1], -ALPHA, None, ALU.mult).then_inc(s_nb, 1)
            step(nc.vector.tensor_tensor(sm[:, 0:1], gmx[:, 0:1], gmx[:, 1:2], ALU.add))
            nc.vector.tensor_scalar(wide[:], sm[:, 0:1], MAX_SPREAD, None, ALU.is_gt).then_inc(s_wide, 1)
            step(nc.vector.tensor_scalar(uu[:, 2, :], sd[:, 0, :], gmx[:, 0:1], None, ALU.add))
            step(nc.vector.scalar_tensor_tensor(nt[:, 0, :], uu[:, 2, :], ALPHA, uu[:, 2, :], ALU.mult, ALU.max))
            nc.vector.tensor_tensor(uu[:, 0, :], uu[:, 2, :], nt[:, 0, :], ALU.subtract)
            nc.vector.scalar_tensor_tensor(uu[:, 1, :], uu[:, 2, :], ALPHA, nt[:, 0, :], ALU.mult,
                                           ALU.subtract).then_inc(s_arg, 1)
            dve.wait_ge(s_exp, 2)
            nc.vector.tensor_tensor(prod, wh[:], bd[:, 0, :].unsqueeze(2).to_broadcast([P, T, FE]),
                                    ALU.mult).then_inc(s_left_b, 1)
            for q in range(PARTS - 1):
                dve.wait_ge(s_part, 2 * q + 1)
                dve.wait_ge(s_left_b, q + 1)
                nc.vector.tensor_tensor(prod, prod, part(0, q), ALU.subtract).then_inc(s_left_b, 1)
            masks(0, 2)
            dve.wait_ge(s_part, 2 * PARTS)
            nc.vector.tensor_scalar(val[:, :, VC:2 * VC], val[:, :, 2 * VC:3 * VC], -1.0, None,
                                    ALU.mult).then_inc(s_minus, 1)
            dve.wait_ge(s_exp, 4)
            dve.wait_ge(s_srowc, G)

            COMBINE = 6

            def combine(p, parity):
                count = [0]

                def link(ins):
                    count[0] += 1
                    ins.then_inc(s_cstep, 1)
                    dve.wait_ge(s_cstep, COMBINE * p + count[0])

                dve.wait_ge(s_mm, U * (p + 1))
                for h in range(2):
                    sums = acc[parity][h][:, 0:4 * VC].rearrange("p (s q c) -> p s c q", s=4, q=PARTS)
                    ins = nc.vector.tensor_reduce(
                        red[:, 2 * h:2 * h + 2, :, :].rearrange("p t s c -> p (t s) c"), sums, AX.X, ALU.add)
                    ins.then_inc(s_comb, 1)
                dve.wait_ge(s_comb, 2 * p + 2)
                link(nc.vector.tensor_tensor(
                    scl[:].rearrange("p t s c -> p (t s) c"), red[:].rearrange("p t s c -> p (t s) c"),
                    ac[:, bass.ts(p, GT), :].rearrange("p t s -> p (t s)").unsqueeze(2).to_broadcast([P, 2 * GT, FE]),
                    ALU.mult))
                link(nc.vector.tensor_tensor(num[:], scl[:, :, 0, :], scl[:, :, 1, :], ALU.add))
                link(nc.vector.tensor_scalar(empty[:], num[:, :, F], NO_WEIGHT, None, ALU.is_lt))
                link(nc.vector.tensor_tensor(scl[:, :, 0, :], wh_sum[:].unsqueeze(1).to_broadcast([P, GT, FE]),
                                             empty[:].unsqueeze(2).to_broadcast([P, GT, FE]), ALU.mult))
                link(nc.vector.tensor_tensor(num[:], num[:], scl[:, :, 0, :], ALU.add))
                link(nc.vector.reciprocal(rden[:], num[:, :, F]))
                at_least(dve, s_hpt, p)
                nc.vector.tensor_tensor(hp[:, :, 0:FE], num[:], rden[:].unsqueeze(2).to_broadcast([P, GT, FE]),
                                        ALU.mult).then_inc(s_hp, 1)
                assert count[0] == COMBINE

            LN2 = 3

            def residual(p, q=None):
                q = p if q is None else q
                count = [0]

                def link(ins):
                    count[0] += 1
                    ins.then_inc(s_lstep, 1)
                    dve.wait_ge(s_lstep, LN2 * p + count[0])

                for h in range(2):
                    dve.wait_ge(s_fc, 2 * p + h + 1)
                    at_least(dve, s_bias, p)
                    nc.vector.tensor_tensor(x1[:, 2 * h:2 * h + 2, :], x_sb[:, bass.ds(GT * q + 2 * h, 2), :],
                                            post[h][:].rearrange("p (t d) -> p t d", d=DIM),
                                            ALU.add).then_inc(s_x1, 1)
                dve.wait_ge(s_x1, 2 * p + 2)
                for u in range(GT):
                    ins = nc.vector.bn_stats(stats[:, u, :], x1[:, u, :])
                link(ins)
                at_least(dve, s_xn, p)
                nc.vector.tensor_copy(sm[:, 0:1], sm[:, 1:2])
                for u in range(GT):
                    ins = nc.vector.bn_aggr(mv2[:, u, :], stats[:, u, :])
                link(ins)
                nc.vector.tensor_scalar(minus_half_v[:], mv2[:, :, 1], EPS, -0.5, ALU.add, ALU.mult)
                link(nc.vector.tensor_scalar(variance[:], mv2[:, :, 1], EPS, None, ALU.add))
                nc.vector.tensor_scalar(rstd2[:].bitcast(I32), variance[:].bitcast(I32), -0.5, float(RSQRT_MAGIC),
                                        ALU.mult, ALU.add).then_inc(s_ln2, 1)
                assert count[0] == LN2

            def normalise(p):
                dve.wait_ge(s_ln2, p + 1)
                newton(rstd2[:], nt[:, 0, 0:GT], variance[:])
                dve.wait_ge(s_xt, KT * p)
                for u in range(GT):
                    ins = nc.vector.tensor_scalar(xn[:, u, :], x1[:, u, :], mv2[:, u, 0:1], rstd2[:, u:u + 1],
                                                  ALU.subtract, ALU.mult)
                ins.then_inc(s_xn, 1)

            def add_mlp(p):
                dve.wait_ge(s_bias, p + 1)
                for h in range(2):
                    dve.wait_ge(s_fc2, 2 * p + h + 1)
                    half = res[:, 2 * h:2 * h + 2, :]
                    nc.vector.tensor_tensor(half, half, post[2 + h][:].rearrange("p (t d) -> p t d", d=DIM),
                                            ALU.add).then_inc(s_out, 1)

            def group(g, parity, one, two):
                for k in range(U):
                    if not isinstance(g, int) or g > 0 or k > 2:
                        masks(g, k)
                    if one is not None:
                        if k == 1:
                            combine(one, 1 - parity)
                        if k == 4:
                            residual(one)
                    if two is not None and k == U - 1:
                        add_mlp(two)

            group(0, 0, None, None)
            dve.wait_ge(s_whsum, 1)
            nc.vector.tensor_copy(wh_sum[:], post[1][:, 0:FE]).then_inc(s_whsumc, 1)
            dve.wait_ge(s_whsumc, 1)
            group(1, 1, 0, None)
            with dve.Fori(2, G - 1, 2) as g:
                group(g, 0, g - 1, g - 2)
                group(g + 1, 1, g, g - 1)
            combine(G - 1, 1)
            residual(G - 1)
            normalise(G - 1)
            add_mlp(G - 2)
            add_mlp(G - 1)

            STEPS = 7

            with exact_pass(dve):
                with dve.Fori(0, G) as c:
                    nc.vector.tensor_tensor(dg[:], ident[:].unsqueeze(1).to_broadcast([P, GT, P]),
                                            sd[:, 1, bass.ts(c, GT)].unsqueeze(2).to_broadcast([P, GT, P]),
                                            ALU.mult).then_inc(s_ediag, 1)
                    dve.wait_ge(s_edst, c + 1)
                    nc.vector.tensor_copy(srow[:, bass.ts(c, GR)], bank[1][:]).then_inc(s_edstc, 1)
                dve.wait_ge(s_edstc, G)
                nc.vector.tensor_copy(neg_max[:, 0:1], gmx[:, 0:1]).then_inc(s_eread, 2)
                dve.wait_ge(s_eread, 2)
                with dve.Fori(0, G) as q:
                    p = q + G
                    for u in range(GT):
                        n = GT * q + u
                        dve.wait_ge(s_efree, n + 1)
                        nc.vector.tensor_tensor(score, srow[:], sd[:, 0, bass.ds(n, 1)].to_broadcast([P, N]),
                                                ALU.add).then_inc(s_estep, 1)
                        dve.wait_ge(s_estep, STEPS * n + 1)
                        nc.vector.scalar_tensor_tensor(score, score, ALPHA, score, ALU.mult,
                                                       ALU.max).then_inc(s_estep, 1)
                        dve.wait_ge(s_estep, STEPS * n + 2)
                        dve.wait_ge(s_erow[u % 2], 16 * (GT // 2 * q + u // 2 + 1))
                        nc.vector.tensor_scalar(limit, row_adj[:, u % 2, :], 0.0, UNBOUND, ALU.is_gt,
                                                ALU.mult).then_inc(s_eread, 1)
                        dve.wait_ge(s_eread, n + 3)
                        nc.vector.scalar_tensor_tensor(score, limit, MASKED, score, ALU.add,
                                                       ALU.min).then_inc(s_estep, 1)
                        dve.wait_ge(s_estep, STEPS * n + 3)
                        nc.vector.tensor_reduce(neg_max[:, 0:1], score, AX.X, ALU.max).then_inc(s_estep, 1)
                        dve.wait_ge(s_estep, STEPS * n + 4)
                        nc.vector.tensor_scalar(neg_max[:, 1:2], neg_max[:, 0:1], -1.0, None,
                                                ALU.mult).then_inc(s_emax, 1)
                        dve.wait_ge(s_esum, n + 1)
                        nc.vector.tensor_copy(red[:, 0, 0, :], bank[0][:, 0:FE]).then_inc(s_estep, 1)
                        dve.wait_ge(s_estep, STEPS * n + 5)
                        nc.vector.reciprocal(rden[:, 0:1], red[:, 0, 0, F:FE]).then_inc(s_estep, 1)
                        dve.wait_ge(s_estep, STEPS * n + 6)
                        if u == 0:
                            dve.wait_ge(s_hpt, p)
                        nc.vector.tensor_scalar(hp[:, u, 0:FE], red[:, 0, 0, :], rden[:, 0:1], None,
                                                ALU.mult).then_inc(s_estep, 1)
                        dve.wait_ge(s_estep, STEPS * n + 7)
                    nc.vector.tensor_copy(hp[:, 0, F:FE], hp[:, 0, F:FE]).then_inc(s_hp, 1)
                    residual(p, q)
                    add_mlp(p)

        @block.tensor
        def _(pe):
            pe.wait_ge(s_w, 64)
            for k in range(KT):
                ins = nc.tensor.matmul(post[0][:, 2 * k:2 * k + 2], wt_sb[:, P * k:P * k + P], a2_sb[:],
                                       start=True, stop=True)
            ins.then_inc(s_wa, 1)
            pe.wait_ge(s_const, CONSTANTS)

            def ln1_transpose(c):
                pe.wait_ge(s_xn1, c + 1)
                at_least(pe, s_xt1c, KT * (c - 1))
                for k in range(KT):
                    for u in range(GT):
                        ins = nc.tensor.transpose(bank[2 * (c % 2) + k][:, P * u:P * u + P],
                                                  ln_rows[c % 2][:, u, P * k:P * k + P], ident[:])
                    ins.then_inc(s_xt1, 1)

            def project(c):
                pe.wait_ge(s_xt1c, KT * c + KT)
                at_least(pe, s_whtc, c - 1)
                for k in range(KT):
                    ins = nc.tensor.matmul(post[c % 2][0:F + 2, :], w_ext[:, k, :], ln_t[c % 2][:, k, :],
                                           start=(k == 0), stop=(k == KT - 1))
                ins.then_inc(s_whp, 1)

            def turn(c):
                pe.wait_ge(s_whtc, c + 1)
                at_least(pe, s_whc, 2 * turn_before(c))
                for u in range(GT):
                    ins = nc.tensor.transpose(turn_banks(c)[0][:, (F + 2) * u:(F + 2) * (u + 1)],
                                              wh_t[:, c, P * u:P * u + P], ident[0:F + 2, 0:F + 2])
                ins.then_inc(s_wh, 1)
                at_least(pe, s_srowc, turn_before(c))
                nc.tensor.matmul(turn_banks(c)[1][:], pick[:], wh_t[:, c, :], start=True, stop=True).then_inc(s_srow, 1)

            ln1_transpose(0)
            pe.wait_ge(s_wext, 1)
            for c in range(G):
                if c >= LAG:
                    turn(c - LAG)
                if c + 1 < G:
                    ln1_transpose(c + 1)
                project(c)
            for c in range(G - LAG, G):
                turn(c)
            pe.wait_ge(s_mx, 1)
            nc.tensor.matmul(post[0][:, 0:2 * P], ones[:], dg[:, 0:2, :].rearrange("p u i -> p (u i)"), start=True,
                             stop=True).then_inc(s_mxb, 1)
            for t in range(T):
                ins = nc.tensor.matmul(post[1][:, 0:FE], ones[:], wh[:, t, :], start=(t == 0), stop=(t == T - 1))
            ins.then_inc(s_whsum, 1)
            pe.wait_ge(s_part, 2 * PARTS)
            pe.wait_ge(s_minus, 1)

            def unit(g, k, parity):
                by_vector, by_scalar = rests(g, k)
                pe.wait_ge(s_pos, U * g + k + 1)
                if k in BY_SCALAR:
                    pe.wait_ge(s_rest_s, by_scalar)
                else:
                    pe.wait_ge(s_rest_v, by_vector)
                if k == 0:
                    at_least(pe, s_comb, 2 * (g - 1))
                pos_columns = 2 * VC if k in BY_SCALAR else VC
                for b in range(UB):
                    j = UB * k + b
                    for u in range(GT):
                        to, col = acc[parity][u // 2], 2 * VC * (u % 2)
                        nc.tensor.matmul(to[:, col:col + pos_columns], pos[:, k % RING, b, P * u:P * u + P],
                                         val[:, j, 0:pos_columns], start=(j == 0 and u % 2 == 0), stop=False,
                                         skip_group_check=True)
                        ins = nc.tensor.matmul(to[:, col + VC:col + 2 * VC], rest[:, k % RING, b, P * u:P * u + P],
                                               val[:, j, 2 * VC:3 * VC], start=False, stop=(j == T - 1),
                                               skip_group_check=True)
                ins.then_inc(s_mm, 1)

            def hp_transpose(p):
                pe.wait_ge(s_hp, p + 1)
                at_least(pe, s_xtc, KT * p)
                for u in range(GT):
                    ins = nc.tensor.transpose(post[0][:, P * u:P * u + P], hp[:, u, :], ident[:])
                ins.then_inc(s_hpt, 1)

            def fc(p):
                pe.wait_ge(s_hptc, p + 1)
                for u in range(GT):
                    ins = nc.tensor.matmul(post[u // 2][:, DIM * (u % 2):DIM * (u % 2 + 1)],
                                           hp_t[:, P * u:P * u + P], fc_sb[:], start=True, stop=True)
                    if u % 2:
                        ins.then_inc(s_fc, 1)

            def ln2_transpose(p):
                pe.wait_ge(s_xn, p + 1)
                for k in range(KT):
                    for u in range(GT):
                        ins = nc.tensor.transpose(post[k][:, P * u:P * u + P], xn[:, u, P * k:P * k + P], ident[:])
                    ins.then_inc(s_xt, 1)

            def fc1(p, m):
                pe.wait_ge(s_xtc, KT * p + KT)
                if m < 2:
                    at_least(pe, s_out, 2 * p - 1 + m)
                else:
                    pe.wait_ge(s_gelu, HT * p + m - 1)
                for k in range(KT):
                    ins = nc.tensor.matmul(post[2 + m % 2][:], fc1_sb[:, k, P * m:P * m + P], x_t[:, k, :],
                                           start=(k == 0), stop=(k == KT - 1))
                ins.then_inc(s_fc1, 1)

            def fc2(p, u):
                pe.wait_ge(s_gelu, HT * p + HT)
                for m in range(HT):
                    ins = nc.tensor.matmul(post[2 + u // 2][:, DIM * (u % 2):DIM * (u % 2 + 1)],
                                           hid[:, m, P * u:P * u + P], fc2_sb[:, m, :], start=(m == 0),
                                           stop=(m == HT - 1))
                if u % 2:
                    ins.then_inc(s_fc2, 1)

            FC2_AT = {3: (0, 1), 4: (2,), 5: (3,)}

            def group(g, parity, one, two):
                for k in range(U):
                    unit(g, k, parity)
                    if one is not None:
                        if k == 1:
                            hp_transpose(one)
                        if k == 2:
                            fc(one)
                        if k == 5:
                            ln2_transpose(one)
                    if two is not None:
                        if k < 2:
                            fc1(two, 2 + k)
                        for u in FC2_AT.get(k, ()):
                            fc2(two, u)
                    if one is not None and k >= 6:
                        fc1(one, k - 6)

            group(0, 0, None, None)
            pe.wait_ge(s_w2, 64)
            group(1, 1, 0, None)
            with pe.Fori(2, G, 2) as g:
                group(g, 0, g - 1, g - 2)
                group(g + 1, 1, g, g - 1)
            p = G - 1
            fc1(p - 1, 2)
            fc1(p - 1, 3)
            hp_transpose(p)
            fc2(p - 1, 0)
            fc(p)
            for u in range(1, GT):
                fc2(p - 1, u)
            ln2_transpose(p)
            for m in range(HT):
                fc1(p, m)
            for u in range(GT):
                fc2(p, u)

            with exact_pass(pe):
                with pe.Fori(0, G) as c:
                    pe.wait_ge(s_ediag, c + 1)
                    nc.tensor.matmul(bank[1][:], ones[:], dg[:].rearrange("p u i -> p (u i)"), start=True,
                                     stop=True).then_inc(s_edst, 1)
                nc.tensor.transpose(bank[0][:, 0:P], ident[:], ident[:]).then_inc(s_efree, 1)
                with pe.Fori(0, G) as q:
                    p = q + G
                    for u in range(GT):
                        n = GT * q + u
                        pe.wait_ge(s_eexp, n + 1)
                        for b in range(T // TB):
                            if b >= 2:
                                pe.wait_ge(s_etrc, T // TB * n + b - 1)
                            for i in range(TB):
                                ins = nc.tensor.transpose(acc[1][b % 2][:, P * i:P * (i + 1)],
                                                          score[:, P * (TB * b + i):P * (TB * b + i + 1)], ident[:])
                            ins.then_inc(s_etr, 1)
                        pe.wait_ge(s_etrc, T // TB * n + T // TB)
                        for j in range(T):
                            ins = nc.tensor.matmul(bank[0][:, 0:FE], score_t[:, P * j:P * (j + 1)], wh[:, j, :],
                                                   start=(j == 0), stop=(j == T - 1))
                        ins.then_inc(s_esum, 1)
                        nc.tensor.transpose(bank[1][:, 0:P], ident[:], ident[:]).then_inc(s_efree, 1)
                    hp_transpose(p)
                    fc(p)
                    ln2_transpose(p)
                    for m in range(HT):
                        fc1(p, m)
                    for i in range(GT):
                        fc2(p, i)


def kernel(x, adj, L0_gnn_W, L0_gnn_a, L0_gnn_fc_w, L0_gnn_fc_b, L0_gnn_ln1_g, L0_gnn_ln1_b, L0_gnn_ln2_g,
           L0_gnn_ln2_b, L0_gnn_fc1_w, L0_gnn_fc1_b, L0_gnn_fc2_w, L0_gnn_fc2_b):
    import numpy as np
    import concourse.bacc as bacc
    from concourse.bass_utils import run_bass_kernel_spmd as run

    nc = bacc.Bacc("TRN2", target_bir_lowering=False, num_devices=1)

    def columns(v):
        return np.asarray(v).reshape(-1, P).T

    adj_t = np.asarray(adj).reshape(G, GR, U, UB, P).transpose(0, 2, 4, 3, 1).reshape(G, U, P, UB * GR)
    arrays = {
        "x": x,
        "adj_t": adj_t,
        "adj_rows": np.asarray(adj).reshape(G, GT, P, N),
        "w": L0_gnn_W,
        "w_t": np.asarray(L0_gnn_W).T,
        "a2": np.asarray(L0_gnn_a).reshape(2, F).T,
        "fc_wt": np.concatenate([np.asarray(L0_gnn_fc_w).T, np.asarray(L0_gnn_fc_b)[None, :]]),
        "fc1_wt": np.asarray(L0_gnn_fc1_w).T,
        "fc2_wt": np.asarray(L0_gnn_fc2_w).T,
        "fc2_b": np.broadcast_to(np.asarray(L0_gnn_fc2_b), (P, DIM)),
        "params": np.concatenate([columns(v) for v in (L0_gnn_ln1_g, L0_gnn_ln1_b, L0_gnn_ln2_g, L0_gnn_ln2_b,
                                                       L0_gnn_fc1_b)], axis=1),
    }
    arrays = {k: np.ascontiguousarray(v) for k, v in arrays.items()}
    dts = {"float32": F32, "int32": I32}
    aps = [nc.dram_tensor(k, v.shape, dts[v.dtype.name], kind="ExternalInput").ap() for k, v in arrays.items()]
    out = nc.dram_tensor("out", (N, DIM), F32, kind="ExternalOutput").ap()
    build(nc, *aps, out)
    r = run(nc, [arrays], core_ids=[0])
    return r.results[0]["out"]
```
